# Optimizing a Trainium2 kernel written in Bass

```python
import numpy as np
import jax
import jax.numpy as jnp

def _softmax(x, axis=-1):
    return jax.nn.softmax(x, axis=axis)

def _gelu(x):
    return jax.nn.gelu(x, approximate=True)

def _silu(x):
    return jax.nn.silu(x)

def _sigmoid(x):
    return jax.nn.sigmoid(x)

def _layernorm(x, axis=-1, eps=1e-05):
    m = jnp.mean(x, axis=axis, keepdims=True)
    v = jnp.var(x, axis=axis, keepdims=True)
    return (x - m) / jnp.sqrt(v + eps)

def _scatter_add(tgt, idx, src, axis=0):
    return tgt.at[idx].add(src)

def _segment_sum(src, seg, n):
    return jax.ops.segment_sum(src, seg, n)
kernel_name = 'mk_adaln_d1_jaxref_r8_c98aa2'

def setup_inputs(seed: int=0):
    np.random.seed(seed)
    _w = jnp.asarray

    def _L0_attn_setup():
        import math
        import jax, jax.numpy as jnp
        import numpy as np
        C = 8.0
        _MIN_RAD, _MAX_RAD = (0.9, 0.999)

        def block_diag_linear(x, w):
            B, T, D = x.shape
            H, bs, _ = w.shape
            xh = x.reshape(B, T, H, bs)
            return jnp.einsum('bthd,hde->bthe', xh, w).reshape(B, T, D)

        def linear_scan(a, b):

            def op(l, r):
                a1, b1 = l
                a2, b2 = r
                return (a1 * a2, a2 * b1 + b2)
            return jax.lax.associative_scan(op, (a, b), axis=1)[1]

        def _reference_tuple_inner(x, a_param, w_in, w_a):
            gate_x = jax.nn.sigmoid(block_diag_linear(x, w_in))
            gate_a = jax.nn.sigmoid(block_diag_linear(x, w_a))
            log_a = -C * jax.nn.softplus(a_param) * gate_a
            a = jnp.exp(log_a)
            multiplier = jnp.sqrt(1.0 - jnp.exp(2.0 * log_a))
            b = multiplier * (gate_x * x)
            y = linear_scan(a, b)
            h_last = y[:, -1, :]
            return (y, h_last)
        key = jax.random.key(seed)
        k1, k2, k3, k4 = jax.random.split(key, 4)
        B, T, D, H = (4, 512, 128, 8)
        bs = D // H
        x = jax.random.normal(k1, (B, T, D), dtype=jnp.float32)
        std = 1.0 / math.sqrt(bs)
        w_in = jax.random.normal(k2, (H, bs, bs), dtype=jnp.float32) * std
        w_a = jax.random.normal(k3, (H, bs, bs), dtype=jnp.float32) * std
        sp = jax.random.uniform(k4, (D,), dtype=jnp.float32, minval=-math.log(_MAX_RAD) / C, maxval=-math.log(_MIN_RAD) / C)
        a_param = jnp.log(jnp.exp(sp) - 1.0 + 1e-08)
        return {'x': x, 'a_param': a_param, 'w_in': w_in, 'w_a': w_a}
    _L0_attn_in = _L0_attn_setup()

    def _L0_ffn_setup():
        import jax, jax.numpy as jnp
        import numpy as np
        EMB, HID, E, TOPK = (128, 512, 8, 2)
        key = jax.random.key(seed)
        ks = jax.random.split(key, 10)
        s = 0.02
        return {'x': jax.random.normal(ks[0], (4, 256, EMB), jnp.float32), 'rw1': s * jax.random.normal(ks[1], (EMB, HID), jnp.float32), 'rb1': jnp.zeros((HID,), jnp.float32), 'rw2': s * jax.random.normal(ks[2], (HID, E), jnp.float32), 'rb2': jnp.zeros((E,), jnp.float32), 'w1': s * jax.random.normal(ks[3], (E, EMB, HID), jnp.float32), 'b1': jnp.zeros((E, HID), jnp.float32), 'w2': s * jax.random.normal(ks[4], (E, HID, EMB), jnp.float32), 'b2': jnp.zeros((E, EMB), jnp.float32)}
    _L0_ffn_in = _L0_ffn_setup()
    _L0_c = _w((lambda *s: np.random.randn(*s).astype(np.float32) * 0.05)(2, 128))
    _L0_wmod = _w((lambda *s: np.random.randn(*s).astype(np.float32) * 0.05)(128, 6 * 128) * 128 ** (-0.5))
    _d = {'L0_attn_x': _L0_attn_in['x'], 'L0_attn_a_param': _L0_attn_in['a_param'], 'L0_attn_w_in': _L0_attn_in['w_in'], 'L0_attn_w_a': _L0_attn_in['w_a'], 'L0_ffn_rw1': _L0_ffn_in['rw1'], 'L0_ffn_rb1': _L0_ffn_in['rb1'], 'L0_ffn_rw2': _L0_ffn_in['rw2'], 'L0_ffn_rb2': _L0_ffn_in['rb2'], 'L0_ffn_w1': _L0_ffn_in['w1'], 'L0_ffn_b1': _L0_ffn_in['b1'], 'L0_ffn_w2': _L0_ffn_in['w2'], 'L0_ffn_b2': _L0_ffn_in['b2'], 'L0_c': _L0_c, 'L0_wmod': _L0_wmod}
    _x0 = _d['L0_attn_x']
    _d['L0_attn_x'] = jax.random.normal(jax.random.fold_in(jax.random.key(seed), 1), (2, 2048, 128), dtype=_x0.dtype)
    del _x0
    return _d

def reference(L0_attn_x, L0_attn_a_param, L0_attn_w_in, L0_attn_w_a, L0_ffn_rw1, L0_ffn_rb1, L0_ffn_rw2, L0_ffn_rb2, L0_ffn_w1, L0_ffn_b1, L0_ffn_w2, L0_ffn_b2, L0_c, L0_wmod):

    def _L0_attn_ref(x, a_param, w_in, w_a):
        import math
        import jax, jax.numpy as jnp
        import numpy as np
        C = 8.0
        _MIN_RAD, _MAX_RAD = (0.9, 0.999)

        def block_diag_linear(x, w):
            B, T, D = x.shape
            H, bs, _ = w.shape
            xh = x.reshape(B, T, H, bs)
            return jnp.einsum('bthd,hde->bthe', xh, w).reshape(B, T, D)

        def linear_scan(a, b):

            def op(l, r):
                a1, b1 = l
                a2, b2 = r
                return (a1 * a2, a2 * b1 + b2)
            return jax.lax.associative_scan(op, (a, b), axis=1)[1]

        def _reference_tuple_inner(x, a_param, w_in, w_a):
            gate_x = jax.nn.sigmoid(block_diag_linear(x, w_in))
            gate_a = jax.nn.sigmoid(block_diag_linear(x, w_a))
            log_a = -C * jax.nn.softplus(a_param) * gate_a
            a = jnp.exp(log_a)
            multiplier = jnp.sqrt(1.0 - jnp.exp(2.0 * log_a))
            b = multiplier * (gate_x * x)
            y = linear_scan(a, b)
            h_last = y[:, -1, :]
            return (y, h_last)
        return _reference_tuple_inner(x, a_param, w_in, w_a)[0]

    def _L0_ffn_ref(x, rw1, rb1, rw2, rb2, w1, b1, w2, b2):
        import jax, jax.numpy as jnp
        import numpy as np
        EMB, HID, E, TOPK = (128, 512, 8, 2)
        B, S, D = x.shape
        logits = jax.nn.silu(jnp.einsum('bsd,dh->bsh', x, rw1) + rb1)
        logits = jnp.einsum('bsh,he->bse', logits, rw2) + rb2
        k_logits, k_index = jax.lax.top_k(logits, TOPK)
        k_prob = jax.nn.softmax(k_logits, axis=-1)
        xf = x.reshape(B * S, D)
        k_index_f = k_index.reshape(B * S, TOPK)
        k_prob_f = k_prob.reshape(B * S, TOPK)
        out = jnp.zeros_like(xf)
        for e in range(E):
            we = jnp.sum(jnp.where(k_index_f == e, k_prob_f, 0.0), axis=-1)
            h = jax.nn.silu(xf @ w1[e] + b1[e]) @ w2[e] + b2[e]
            out = out + we[:, None] * h
        return out.reshape(B, S, D)
    x = L0_attn_x
    mod = (_silu(L0_c) @ L0_wmod).reshape(L0_c.shape[0], 6, 1, -1)
    sa, ca, ga, sb, cb, gb = (mod[:, 0], mod[:, 1], mod[:, 2], mod[:, 3], mod[:, 4], mod[:, 5])
    ga = (2 * (ga >= 0) - 1) * jnp.maximum(jnp.abs(ga), 0.25)
    gb = (2 * (gb >= 0) - 1) * jnp.maximum(jnp.abs(gb), 0.25)
    h = _layernorm(x, axis=-1) * (1 + ca) + sa
    x = x + ga * _L0_attn_ref(h, L0_attn_a_param, L0_attn_w_in, L0_attn_w_a)
    h = _layernorm(x, axis=-1) * (1 + cb) + sb
    x = x + gb * _L0_ffn_ref(h, L0_ffn_rw1, L0_ffn_rb1, L0_ffn_rw2, L0_ffn_rb2, L0_ffn_w1, L0_ffn_b1, L0_ffn_w2, L0_ffn_b2)
    return x

_drawn_inputs = setup_inputs


def setup_inputs(seed=0):
    import zlib

    import numpy as np

    out = dict(_drawn_inputs(seed))
    spreads = {'L0_ffn_rb1': (0.0, 0.8),
     'L0_ffn_rb2': (0.0, 0.446),
     'L0_ffn_b1': (0.0, 0.8),
     'L0_ffn_b2': (0.0, 0.49)}
    factors = {'L0_ffn_rw1': 4.696, 'L0_ffn_rw2': 4.542, 'L0_ffn_w1': 6.236, 'L0_ffn_w2': 5.597}
    for name, (base, spread) in spreads.items():
        noise = np.random.default_rng([zlib.crc32(name.encode()), seed]).standard_normal(out[name].shape)
        drawn = base * np.exp(spread * noise) if base else spread * noise
        out[name] = jnp.asarray(drawn.astype(out[name].dtype))
    for name, factor in factors.items():
        out[name] = (out[name] * factor).astype(out[name].dtype)
    return out
```

```python
from contextlib import ExitStack

import concourse.bass as bass
from concourse import mybir

ALU = mybir.AluOpType
ACT = mybir.ActivationFunctionType
AX = mybir.AxisListType
F32 = mybir.dt.float32
BF16 = mybir.dt.bfloat16
I32 = mybir.dt.int32

P = 128
EPS = 1e-5
GATE_FLOOR = 0.25
NEG_HUGE = -3.0e38
EULER = 2.718281828459045


def adaln_block(nc, x, a_param, w_in, w_a, rw1, rb1, rw2, rb2, w1, b1, w2, b2, c, wmod, out):
    B, T, D = x.shape
    NH, HB, _ = w_in.shape
    HID = rw1.shape[1]
    NE = rw2.shape[1]
    TOK = B * T
    NT = TOK // P
    GT = 4
    G = GT * P
    NG = TOK // G
    GPB = NG // B
    HC = HID // P
    TOPK = 2
    REG = TOK + P
    ROW = D + 2
    U = 8
    TILES = -(-(TOPK * TOK // P + NE - 1) // U) * U
    KT = NT
    assert D == P and HC == GT and B == 2 and TILES == 72

    x_t = x.rearrange("b (n p) d -> p (b n) d", p=P)
    out_t = out.rearrange("b (n p) d -> p (b n) d", p=P)

    with ExitStack() as ctx:
        def sb(name, shape, dt=F32):
            return ctx.enter_context(nc.sbuf_tensor(name, shape, dt))

        def ps(name, shape, dt=F32):
            return ctx.enter_context(nc.psum_tensor(name, shape, dt))

        def sem(name):
            return ctx.enter_context(nc.semaphore(name))

        sorted_rows = nc.dram_tensor("sorted_rows", [NE * REG + P, ROW], F32)
        expert_out = nc.dram_tensor("expert_out", [TOPK * TOK, D], F32)

        xs = sb("xs", [P, NT, D])
        wx_bd = sb("wx_bd", [P, P])
        wa_bd = sb("wa_bd", [P, P])
        rw1_s = sb("rw1_s", [P, HID])
        rw2_s = sb("rw2_s", [P, HC, NE])
        rb1_s = sb("rb1_s", [P, HC])
        rb2_s = sb("rb2_s", [1, NE])
        w1_s = sb("w1_s", [P, NE * HID])
        w2_s = sb("w2_s", [P, NE * HC * D])
        wmod_s = sb("wmod_s", [P, 6 * D])
        cT = sb("cT", [P, B])
        csil = sb("csil", [P, 3, B])
        csil_b = sb("csil_b", [P, B, P])
        apar = sb("apar", [P, 1])
        softp = sb("softp", [P, 8])
        modc = sb("modc", [P, 6, B])
        gac = sb("gac", [P, 3, B])
        sbB = sb("sbB", [P, B, D])
        cbB = sb("cbB", [P, B, D])
        gbB = sb("gbB", [P, B, D])
        gbS = sb("gbS", [P, B, D])
        ident = sb("ident", [P, P])
        before = sb("before", [P, P], BF16)
        ones_bf = sb("ones_bf", [P, P], BF16)
        ones_row = sb("ones_row", [1, P])
        half_neg = sb("half_neg", [P, GT])
        euler = sb("euler", [P, GT])
        b1_in = sb("b1_in", [P, NE * HID // P])
        b2_in = sb("b2_in", [P, NE * D // P])
        b1_r = sb("b1_r", [P, 2, NE * HID // P])
        b2_r = sb("b2_r", [P, 2, NE * D // P])
        b1_p = sb("b1_p", [P, 3, NE * HID // P], BF16)
        b2_p = sb("b2_p", [P, 3, NE * D // P], BF16)
        b1_s = sb("b1_s", [3, NE * HID], BF16)
        b2_s = sb("b2_s", [3, NE * D], BF16)
        st1 = sb("st1", [P, NT, 6])
        mv1 = sb("mv1", [P, NT, 2])
        ve1 = sb("ve1", [P, NT])
        rs1 = sb("rs1", [P, NT])
        st2 = sb("st2", [P, NT, 6])
        mv2 = sb("mv2", [P, NT, 2])
        ve2 = sb("ve2", [P, NT])
        rs2 = sb("rs2", [P, NT])
        xn = sb("xn", [P, 2, GT, D])
        hT = sb("hT", [P, TOK])
        tx = sb("tx", [P, TOK])
        ta = sb("ta", [P, 2, G])
        av = sb("av", [P, TOK])
        qv = sb("qv", [P, TOK])
        yv = hT
        rows = sb("rows", [P, NT, TOPK, ROW])
        h2T = sb("h2T", [P, 2, G])
        hr = [z[:, 0:HC * G].rearrange("p (h t) -> p h t", h=HC) for z in (av, qv)]
        iota_i = sb("iota_i", [P, 256], I32)
        eid = sb("eid", [P, GT, NE])
        eid8 = sb("eid8", [P, GT, NE])
        ereg = sb("ereg", [P, GT, NE])
        lg = sb("lg", [P, GT, NE])
        t1 = sb("t1", [P, GT, NE])
        t2 = sb("t2", [P, GT, NE])
        mk = sb("mk", [P, TOPK, GT, NE])
        best = sb("best", [P, TOPK, GT])
        bidx = sb("bidx", [P, TOPK, GT])
        mboth = sb("mboth", [P, NT, NE], BF16)
        mcum = sb("mcum", [P, NG + 1, NE])
        mcum_b = sb("mcum_b", [P, NG + 1, NE], BF16)
        msum = sb("msum", [P, NE])
        dlt = sb("dlt", [P, 2, GT])
        edl = sb("edl", [P, 2, GT])
        prb = sb("prb", [P, 2, GT])
        slots = sb("slots", [P, GT, NE])
        slotf = sb("slotf", [P, TOPK, NT])
        sloti = sb("sloti", [P, TOPK, NT], I32)
        padr = sb("padr", [P, ROW])
        cf = sb("cf", [1, NE])
        k128 = sb("k128", [1, KT])
        tauf = sb("tauf", [1, TILES])
        cmpk = sb("cmpk", [1, NE, KT])
        te = sb("te", [1, NE])
        sinc = sb("sinc", [1, NE])
        one8 = sb("one8", [1, NE])
        cmpt = sb("cmpt", [1, TILES, NE])
        cmpu = sb("cmpu", [1, TILES, NE])
        tf = sb("tf", [1, 5, TILES])
        tab_row = sb("tab_row", [1, TILES], I32)
        tab_e = sb("tab_e", [1, TILES], I32)
        pad_f = sb("pad_f", [1, NE])
        pad_i = sb("pad_i", [1, NE], I32)
        spare = [0]

        def in_tx(n):
            spare[0] += n
            assert spare[0] <= TOK
            return tx[:, spare[0] - n:spare[0]]

        xr = in_tx(U * ROW).rearrange("p (u r) -> p u r", u=U)
        xT = in_tx(2 * P).rearrange("p (r t) -> p r t", r=2)
        hs = in_tx(2 * HID).rearrange("p (r h) -> p r h", r=2)
        hsT = in_tx(2 * HID).rearrange("p (r c t) -> p r c t", r=2, c=HC)
        yo = in_tx(4 * D).rearrange("p (r d) -> p r d", r=4)
        y01 = av[:, 0:2 * TOPK * G].rearrange("p (r k n d) -> p r k n d", r=2, k=TOPK, d=D)
        fo = qv[:, 0:4 * G].rearrange("p (r k n d) -> p r k n d", r=2, k=2, d=D)

        bank = [ps(f"bank{i}", [P, 512]) for i in range(8)]

        s_x = [sem(f"s_x{g}") for g in range(NG)]
        s_wsm = sem("s_wsm")
        s_wbd = sem("s_wbd")
        s_rw = sem("s_rw")
        s_w1 = sem("s_w1")
        s_w2 = sem("s_w2")
        s_bin = sem("s_bin")
        s_bs = sem("s_bs")
        s_const = sem("s_const")
        s_pz = sem("s_pz")
        s_dve = sem("s_dve")
        s_ecs = sem("s_ecs")
        s_esp = sem("s_esp")
        s_absa = sem("s_absa")
        s_cs = sem("s_cs")
        s_modc = sem("s_modc")
        s_modb = sem("s_modb")
        s_modok = sem("s_modok")
        s_bp = sem("s_bp")
        s_var1 = sem("s_var1")
        s_rstd1 = sem("s_rstd1")
        s_xn = sem("s_xn")
        s_xnT = sem("s_xnT")
        s_hT = sem("s_hT")
        s_z = sem("s_z")
        s_tanh = sem("s_tanh")
        s_ta = sem("s_ta")
        s_exp = sem("s_exp")
        s_u = sem("s_u")
        s_m = sem("s_m")
        s_y = sem("s_y")
        s_yT = sem("s_yT")
        s_var2 = sem("s_var2")
        s_rstd2 = sem("s_rstd2")
        s_h2 = sem("s_h2")
        s_h2t = sem("s_h2t")
        s_h2T = sem("s_h2T")
        s_dup = sem("s_dup")
        s_rl1 = sem("s_rl1")
        s_hr = sem("s_hr")
        s_lg = sem("s_lg")
        s_lgc = sem("s_lgc")
        s_mask = sem("s_mask")
        s_pos = sem("s_pos")
        s_dlt = sem("s_dlt")
        s_edl = sem("s_edl")
        s_slot = sem("s_slot")
        s_disp = sem("s_disp")
        s_cnt = sem("s_cnt")
        s_tab = sem("s_tab")
        s_pad = sem("s_pad")
        s_xr = [sem(f"s_xr{i}") for i in range(U)]
        s_txp = sem("s_txp")
        s_xT = sem("s_xT")
        s_l1 = sem("s_l1")
        s_hs = sem("s_hs")
        s_thp = sem("s_thp")
        s_hsT = sem("s_hsT")
        s_l2 = sem("s_l2")
        s_yo = sem("s_yo")
        s_sc = [sem(f"s_sc{i}") for i in range(U)]
        s_y01 = [sem(f"s_y01{i}") for i in range(2)]
        s_fin = sem("s_fin")
        s_out = [sem(f"s_out{i}") for i in range(2)]

        rows_i = rows[:, :, :, :].bitcast(I32)
        padr_i = padr[:, :].bitcast(I32)
        xr_i = xr.bitcast(I32)
        block = ctx.enter_context(nc.Block())

        def cols(g):
            return slice(g * G, (g + 1) * G)

        def tiles(g):
            return slice(g * GT, (g + 1) * GT)

        def expert_steps(eng, body, last):
            for s in range(U):
                body(s, s)
            with eng.Fori(1, TILES // U) as n:
                for u in range(U):
                    body(n * U + u, u)
            for s in range(TILES, last):
                body(s, s % U)

        def expert_steps_skewed(eng, body):
            for s in range(U):
                body(s, s)
            with eng.Fori(1, TILES // U - 1) as n:
                for u in range(U):
                    body(n * U + u, u)
            for s in range(TILES - U, TILES + 2):
                body(s, s % U)

        def rounds(s):
            return s // U + 1

        @block.sync
        def _(sp):
            for g in range(NG):
                sp.dma_start(xs[:, tiles(g), :], x_t[:, tiles(g), :]).then_inc(s_x[g], 16)
                if g == 1:
                    sp.dma_start(rw1_s[:, :], rw1).then_inc(s_rw, 16)
                    sp.dma_start(rw2_s[:, :, :], rw2.rearrange("(c p) e -> p c e", p=P)).then_inc(s_rw, 16)
            sp.dma_start(rb2_s[:, :], rb2.rearrange("(a e) -> a e", a=1)).then_inc(s_rw, 16)
            sp.wait_ge(s_bp, 1)
            for k in range(3):
                sp.dma_start(b1_s[k:k + 1, :], b1_p[:, k, :]).then_inc(s_bs, 16)
                sp.dma_start(b2_s[k:k + 1, :], b2_p[:, k, :]).then_inc(s_bs, 16)
            for e in range(NE):
                sp.dma_start(w1_s[:, e * HID:(e + 1) * HID], w1[e]).then_inc(s_w1, 16)
                sp.dma_start(w2_s[:, e * HC * D:(e + 1) * HC * D].rearrange("p (c d) -> p c d", c=HC),
                             w2[e].rearrange("(c p) d -> p c d", p=P)).then_inc(s_w2, 16)
            sp.wait_ge(s_const, 9)
            sp.dma_start(sorted_rows[NE * REG:NE * REG + P, :], padr[:, :]).then_inc(s_pad, 16)
            sp.wait_ge(s_tab, 1)
            for e in range(NE):
                r = sp.value_load(pad_i[0:1, e:e + 1], min_val=e * REG, max_val=e * REG + TOK)
                sp.dma_start(sorted_rows[bass.ds(r, P), :], padr[:, :]).then_inc(s_pad, 16)
            sp.wait_ge(s_pad, 16 * (NE + 1))
            sp.wait_ge(s_disp, 16 * TOPK * NT)

            def load(s, u):
                r = sp.value_load(tab_row[0:1, bass.ds(s, 1)], min_val=0, max_val=NE * REG)
                if not (isinstance(s, int) and s < U):
                    sp.wait_ge(s_sc[u], 16 * (rounds(s) - 1))
                sp.dma_start(xr[:, u, :], sorted_rows[bass.ds(r, P), :]).then_inc(s_xr[u], 16)

            expert_steps(sp, load, TILES)
            for u in range(U):
                sp.wait_ge(s_sc[u], 16 * (TILES // U))
            for g in range(NG):
                if g >= 2:
                    sp.wait_ge(s_fin, g - 1)
                for k in range(TOPK):
                    sp.dma_start(y01[:, g % 2, k, :, :],
                                 expert_out[k * TOK + g * G:k * TOK + (g + 1) * G, :]
                                 .rearrange("(n p) d -> p n d", p=P)).then_inc(s_y01[g % 2], 16)

        @block.gpsimd
        def _(pool):
            nc.gpsimd.memset(wx_bd[:, :], 0.0).then_inc(s_pz, 1)
            nc.gpsimd.memset(wa_bd[:, :], 0.0).then_inc(s_pz, 1)
            nc.gpsimd.memset(half_neg[:, :], -0.5).then_inc(s_const, 1)
            nc.gpsimd.memset(ident[:, :], 0.0).then_inc(s_pz, 1)
            nc.gpsimd.memset(before[:, :], 1.0).then_inc(s_pz, 1)
            pool.wait_ge(s_pz, 4)
            nc.gpsimd.affine_select(out=ident[:, :], in_=ident[:, :], compare_op=ALU.not_equal, fill=1.0,
                                    base=0, pattern=[[-1, P]], channel_multiplier=1).then_inc(s_const, 1)
            nc.gpsimd.affine_select(out=before[:, :], in_=before[:, :], compare_op=ALU.is_gt, fill=0.0,
                                    base=0, pattern=[[1, P]], channel_multiplier=-1).then_inc(s_const, 1)

            def rstd1(g):
                pool.wait_ge(s_var1, g + 1)
                nc.gpsimd.tensor_tensor(rs1[:, tiles(g)], ve1[:, tiles(g)], half_neg[:, :],
                                        ALU.pow).then_inc(s_rstd1, 1)

            rstd1(0)
            rstd1(1)
            nc.gpsimd.memset(ones_bf[:, :], 1.0).then_inc(s_const, 1)
            nc.gpsimd.memset(ones_row[:, :], 1.0).then_inc(s_const, 1)
            nc.gpsimd.memset(euler[:, :], EULER).then_inc(s_const, 1)
            nc.gpsimd.iota(iota_i[:, 0:GT * NE], pattern=[[0, GT], [1, NE]], base=0,
                           channel_multiplier=0).then_inc(s_const, 1)
            rstd1(2)
            for k in range(TOPK):
                ins = nc.gpsimd.iota(rows_i[:, :, k, D + 1], pattern=[[P, NT]], base=k * TOK, channel_multiplier=1)
            ins.then_inc(s_const, 1)
            nc.gpsimd.memset(padr[:, :], 0.0).then_inc(s_pz, 1)
            pool.wait_ge(s_pz, 5)
            nc.gpsimd.iota(padr_i[:, D + 1:D + 2], pattern=[[0, 1]], base=TOPK * TOK,
                           channel_multiplier=1).then_inc(s_const, 1)
            nc.gpsimd.iota(iota_i[0:1, 64:64 + KT], pattern=[[P, KT]], base=0,
                           channel_multiplier=0).then_inc(s_const, 1)
            nc.gpsimd.iota(iota_i[0:1, 128:128 + TILES], pattern=[[1, TILES]], base=0,
                           channel_multiplier=0).then_inc(s_const, 1)
            for g in range(3, NG):
                rstd1(g)

            def rstd2(g):
                pool.wait_ge(s_var2, g + 1)
                nc.gpsimd.tensor_tensor(rs2[:, tiles(g)], ve2[:, tiles(g)], half_neg[:, :],
                                        ALU.pow).then_inc(s_rstd2, 1)

            def exp_delta(g):
                pool.wait_ge(s_dlt, g + 1)
                nc.gpsimd.tensor_tensor(edl[:, g % 2, :], euler[:, :], dlt[:, g % 2, :],
                                        ALU.pow).then_inc(s_edl, 1)

            def dispatch(g):
                pool.wait_ge(s_slot, g + 1)
                pool.wait_ge(s_dup, g + 1)
                for t in range(g * GT, (g + 1) * GT):
                    for k in range(TOPK):
                        nc.gpsimd.indirect_dma_start(
                            sorted_rows[:, :], bass.IndirectOffsetOnAxis(ap=sloti[:, k, t:t + 1], axis=0),
                            rows[:, t, k, :], None).then_inc(s_disp, 16)

            rstd2(0)
            rstd2(1)
            for g in range(NG):
                if g + 2 < NG:
                    rstd2(g + 2)
                exp_delta(g)
                dispatch(g)

            last_row = pool.to_reg(TOPK * TOK - 1)

            def scatter(s, u):
                pool.wait_ge(s_yo, s + 1)
                nc.gpsimd.indirect_dma_start(
                    expert_out[:, :], bass.IndirectOffsetOnAxis(ap=xr_i[:, u, D + 1:D + 2], axis=0),
                    yo[:, u % 4, :], None, bounds_check=last_row, oob_is_err=False).then_inc(s_sc[u], 16)

            for s in range(TILES):
                scatter(s, s % U)

        @block.scalar
        def _(act):
            act.dma_start(wmod_s[:, :], wmod).then_inc(s_wsm, 16)
            with nc.allow_non_contiguous_dma(reason="a few hundred elements"):
                act.dma_start(cT[:, :], c.rearrange("b p -> p b")).then_inc(s_wsm, 16)
                act.dma_start(apar[:, :], a_param.rearrange("(p a) -> p a", a=1)).then_inc(s_wsm, 16)
                act.dma_start(rb1_s[:, :], rb1.rearrange("(c p) -> p c", p=P)).then_inc(s_rw, 16)
            act.wait_ge(s_pz, 2)
            for h in range(NH):
                d = slice(h * HB, (h + 1) * HB)
                act.dma_start(wx_bd[d, d], w_in[h]).then_inc(s_wbd, 16)
                act.dma_start(wa_bd[d, d], w_a[h]).then_inc(s_wbd, 16)
            act.dma_start(b1_in[:, :], b1.rearrange("e (q n) -> (e q) n", q=P // NE)).then_inc(s_bin, 16)
            act.dma_start(b2_in[:, :], b2.rearrange("e (q n) -> (e q) n", q=P // NE)).then_inc(s_bin, 16)
            act.wait_ge(s_wsm, 48)
            nc.scalar.activation(csil[:, 0, :], cT[:, :], ACT.Exp, scale=-1.0).then_inc(s_ecs, 1)
            act.wait_ge(s_absa, 1)
            nc.scalar.activation(softp[:, 1:2], softp[:, 0:1], ACT.Exp, scale=-1.0).then_inc(s_esp, 1)

            def modulate(g):
                act.wait_ge(s_xnT, g + 1)
                if g == 0:
                    act.wait_ge(s_modok, 1)
                b = g // GPB
                nc.scalar.activation(hT[:, cols(g)], bank[g % 2][:, :], ACT.Identity,
                                     bias=modc[:, 0, b:b + 1], scale=gac[:, 0, b:b + 1]).then_inc(s_hT, 1)

            def gates(g):
                act.wait_ge(s_z, g + 1)
                nc.scalar.activation(tx[:, cols(g)], bank[2][:, :], ACT.Tanh, scale=0.5).then_inc(s_tanh, 1)
                nc.scalar.activation(ta[:, g % 2, :], bank[3][:, :], ACT.Tanh, scale=0.5).then_inc(s_ta, 1)

            def decay(g):
                if g == 0:
                    act.wait_ge(s_modok, 2)
                act.wait_ge(s_ta, g + 1)
                nc.scalar.activation(av[:, cols(g)], ta[:, g % 2, :], ACT.Exp, bias=softp[:, 6:7],
                                     scale=softp[:, 6:7])
                nc.scalar.activation(qv[:, cols(g)], ta[:, g % 2, :], ACT.Exp, bias=softp[:, 7:8],
                                     scale=softp[:, 7:8]).then_inc(s_exp, 1)

            def multiplier(g):
                act.wait_ge(s_u, g + 1)
                nc.scalar.activation(qv[:, cols(g)], qv[:, cols(g)], ACT.Sqrt, bias=gac[:, 2, 0:1],
                                     scale=-0.25).then_inc(s_m, 1)

            modulate(0)
            modulate(1)
            for g in range(NG):
                gates(g)
                decay(g)
                if g + 2 < NG:
                    modulate(g + 2)
                if g % GPB == GPB - 1:
                    for j in range(g - GPB + 1, g + 1):
                        multiplier(j)

            def router_copy(g):
                act.wait_ge(s_h2t, g + 1)
                if g >= 2:
                    act.wait_ge(s_rl1, HC * (g - 1))
                nc.scalar.copy(h2T[:, g % 2, :], bank[g % 2][:, :]).then_inc(s_h2T, 1)
                nc.scalar.copy(rows[:, tiles(g), 1, 0:D], rows[:, tiles(g), 0, 0:D]).then_inc(s_dup, 1)

            def router_silu(g):
                if g >= 2:
                    act.wait_ge(s_lg, g - 1)
                for h in range(HC):
                    act.wait_ge(s_rl1, HC * g + h + 1)
                    nc.scalar.activation(hr[g % 2][:, h, :], bank[2 + h % 2][:, :], ACT.Silu,
                                         bias=rb1_s[:, h:h + 1]).then_inc(s_hr, 1)

            act.wait_ge(s_rw, 64)
            router_copy(0)
            for g in range(NG):
                if g + 1 < NG:
                    router_copy(g + 1)
                router_silu(g)

            def hidden(s, u):
                act.wait_ge(s_l1, s + 1)
                if not (isinstance(s, int) and s < 2):
                    act.wait_ge(s_thp, s - 1)
                nc.scalar.activation(hs[:, u % 2, :], bank[2 + u % 2][:, :], ACT.Silu).then_inc(s_hs, 1)

            expert_steps(act, hidden, TILES)

            for g in range(NG):
                act.wait_ge(s_fin, g + 1)
                act.dma_start(out_t[:, tiles(g), :], fo[:, g % 2, 1, :, :]).then_inc(s_out[g % 2], 16)
            for i in range(2):
                act.wait_ge(s_out[i], 16 * (NG // 2))

        @block.vector
        def _(dve):
            chain = [0]

            def link(ins):
                chain[0] += 1
                ins.then_inc(s_dve, 1)
                dve.wait_ge(s_dve, chain[0])

            v = nc.vector

            def stats(st, mv, ve, g, done):
                for t in range(g * GT, (g + 1) * GT):
                    ins = v.bn_stats(st[:, t, :], xs[:, t, :])
                link(ins)
                for t in range(g * GT, (g + 1) * GT):
                    ins = v.bn_aggr(mv[:, t, :], st[:, t, :])
                link(ins)
                v.tensor_scalar(ve[:, tiles(g)], mv[:, tiles(g), 1], EPS, None, ALU.add).then_inc(done, 1)

            def ln1_stats(g):
                dve.wait_ge(s_x[g], 16)
                stats(st1, mv1, ve1, g, s_var1)

            def ln1_norm(g):
                dve.wait_ge(s_rstd1, g + 1)
                if g >= 2:
                    dve.wait_ge(s_xnT, g - 1)
                for j in range(GT):
                    t = g * GT + j
                    ins = v.tensor_scalar(xn[:, g % 2, j, :], xs[:, t, :], mv1[:, t, 0:1], rs1[:, t:t + 1],
                                          ALU.subtract, ALU.mult)
                ins.then_inc(s_xn, 1)

            ln1_stats(0)
            ln1_stats(1)
            dve.wait_ge(s_wsm, 48)
            v.scalar_tensor_tensor(softp[:, 0:1], apar[:, :], -1.0, apar[:, :], ALU.mult, ALU.max).then_inc(s_absa, 1)
            dve.wait_ge(s_ecs, 1)
            link(v.tensor_scalar(csil[:, 1, :], csil[:, 0, :], 1.0, None, ALU.add))
            link(v.reciprocal(csil[:, 2, :], csil[:, 1, :]))
            link(v.tensor_tensor(csil[:, 0, :], cT[:, :], csil[:, 2, :], ALU.mult))
            v.tensor_copy(csil_b[:, :, :], csil[:, 0, :].unsqueeze(2).to_broadcast([P, B, P])).then_inc(s_cs, 1)
            ln1_norm(0)
            dve.wait_ge(s_modc, 1)
            link(v.tensor_copy(modc[:, :, :], bank[6][:, 0:6 * B].rearrange("p (i b) -> p i b", b=B)))
            v.memset(gac[:, 2, :], 0.25)
            v.tensor_scalar(gac[:, 0, :], modc[:, 1, :], 1.0, None, ALU.add).then_inc(s_modok, 1)
            link(v.tensor_scalar(gac[:, 1, :], modc[:, 2, :], 0.0, 2.0, ALU.is_ge, ALU.mult))
            link(v.scalar_tensor_tensor(modc[:, 2, :], modc[:, 2, :], -1.0, modc[:, 2, :], ALU.mult, ALU.max))
            link(v.tensor_scalar(modc[:, 2, :], modc[:, 2, :], GATE_FLOOR, None, ALU.max))
            link(v.scalar_tensor_tensor(gac[:, 1, :], gac[:, 1, :], -1.0, modc[:, 2, :], ALU.add, ALU.mult))
            ln1_norm(1)
            dve.wait_ge(s_esp, 1)
            link(v.tensor_scalar(softp[:, 2:3], softp[:, 1:2], 2.0, None, ALU.add))
            link(v.reciprocal(softp[:, 3:4], softp[:, 2:3]))
            link(v.tensor_tensor(softp[:, 2:3], softp[:, 1:2], softp[:, 3:4], ALU.mult))
            link(v.tensor_tensor(softp[:, 3:4], softp[:, 2:3], softp[:, 2:3], ALU.mult))
            link(v.tensor_scalar(softp[:, 4:5], softp[:, 3:4], 1 / 17, 1 / 15, ALU.mult, ALU.add))
            for k in range(13, 0, -2):
                link(v.tensor_scalar(softp[:, 4:5], softp[:, 4:5], softp[:, 3:4], 1 / k, ALU.mult, ALU.add))
            link(v.tensor_scalar(softp[:, 5:6], apar[:, :], 0.0, 0.5, ALU.max, ALU.mult))
            link(v.tensor_scalar(softp[:, 4:5], softp[:, 4:5], softp[:, 2:3], softp[:, 5:6], ALU.mult, ALU.add))
            v.tensor_scalar(softp[:, 6:7], softp[:, 4:5], -8.0, None, ALU.mult)
            v.tensor_scalar(softp[:, 7:8], softp[:, 4:5], -16.0, None, ALU.mult).then_inc(s_modok, 1)

            def inputs_u(g):
                dve.wait_ge(s_exp, g + 1)
                v.tensor_scalar(qv[:, cols(g)], qv[:, cols(g)], 1.0, None, ALU.min).then_inc(s_u, 1)
                v.scalar_tensor_tensor(tx[:, cols(g)], tx[:, cols(g)], 1.0, hT[:, cols(g)],
                                       ALU.add, ALU.mult)

            def scan(g):
                b = g // GPB
                dve.wait_ge(s_m, g + 1)
                link(v.scalar_tensor_tensor(tx[:, cols(g)], tx[:, cols(g)], gac[:, 1, b:b + 1], qv[:, cols(g)],
                                            ALU.mult, ALU.mult))
                if g % GPB:
                    dve.wait_ge(s_y, g)
                init = 0.0 if g % GPB == 0 else yv[:, g * G - 1:g * G]
                v.tensor_tensor_scan(yv[:, cols(g)], av[:, cols(g)], tx[:, cols(g)], init,
                                     ALU.mult, ALU.add).then_inc(s_y, 1)

            def residual(g):
                dve.wait_ge(s_yT, g + 1)
                link(v.tensor_tensor(xs[:, tiles(g), :], bank[4 + g % 2][:, :].rearrange("p (n d) -> p n d", d=D),
                                     xs[:, tiles(g), :], ALU.add))

            def ln2_norm(g):
                b = g // GPB
                dve.wait_ge(s_rstd2, g + 1)
                if g == 0:
                    dve.wait_ge(s_modok, 3)
                for j in range(GT):
                    t = g * GT + j
                    ins = v.scalar_tensor_tensor(rows[:, t, 0, 0:D], xs[:, t, :], mv2[:, t, 0:1], cbB[:, b, :],
                                                 ALU.subtract, ALU.mult)
                link(ins)
                for j in range(GT):
                    t = g * GT + j
                    ins = v.scalar_tensor_tensor(rows[:, t, 0, 0:D], rows[:, t, 0, 0:D], rs2[:, t:t + 1],
                                                 sbB[:, b, :], ALU.mult, ALU.add)
                ins.then_inc(s_h2, 1)

            def top2(g):
                dve.wait_ge(s_lg, g + 1)
                v.tensor_copy(lg[:, :, :], bank[6][:, 0:GT * NE].rearrange("p (j e) -> p j e", e=NE)).then_inc(s_lgc, 1)
                dve.wait_ge(s_lgc, g + 1)
                for k in range(TOPK):
                    link(v.tensor_reduce(best[:, k, :], lg[:, :, :], AX.X, ALU.max))
                    link(v.tensor_tensor(t1[:, :, :], lg[:, :, :],
                                         best[:, k, :].unsqueeze(2).to_broadcast([P, GT, NE]), ALU.is_ge))
                    link(v.scalar_tensor_tensor(t2[:, :, :], t1[:, :, :], -float(NE), eid8[:, :, :],
                                                ALU.mult, ALU.add))
                    link(v.tensor_reduce(bidx[:, k, :], t2[:, :, :], AX.X, ALU.min))
                    link(v.tensor_tensor(mk[:, k, :, :], eid[:, :, :],
                                         bidx[:, k, :].unsqueeze(2).to_broadcast([P, GT, NE]), ALU.is_equal))
                    if k == 0:
                        link(v.scalar_tensor_tensor(lg[:, :, :], mk[:, 0, :, :], NEG_HUGE, lg[:, :, :],
                                                    ALU.mult, ALU.add))
                v.tensor_tensor(dlt[:, g % 2, :], best[:, 1, :], best[:, 0, :], ALU.subtract).then_inc(s_dlt, 1)
                link(v.tensor_tensor(mboth[:, tiles(g), :], mk[:, 0, :, :], mk[:, 1, :, :], ALU.add))
                link(v.tensor_reduce(msum[:, :], mboth[:, tiles(g), :].rearrange("p j e -> p e j"), AX.X, ALU.add))
                link(v.tensor_tensor(mcum[:, g + 1, :], mcum[:, g, :], msum[:, :], ALU.add))
                v.tensor_copy(mcum_b[:, g + 1, :], mcum[:, g + 1, :]).then_inc(s_mask, 1)
                dve.wait_ge(s_edl, g + 1)
                link(v.tensor_scalar(prb[:, 0, :], edl[:, g % 2, :], 1.0, None, ALU.add))
                link(v.reciprocal(prb[:, 1, :], prb[:, 0, :]))
                v.tensor_copy(rows[:, tiles(g), 0, D], prb[:, 1, :])
                v.tensor_tensor(rows[:, tiles(g), 1, D], edl[:, g % 2, :], prb[:, 1, :], ALU.mult)
                dve.wait_ge(s_pos, g + 1)
                link(v.tensor_tensor(slots[:, :, :], bank[7][:, 0:GT * NE].rearrange("p (j e) -> p j e", e=NE),
                                     ereg[:, :, :], ALU.add))
                link(v.tensor_tensor(t1[:, :, :], slots[:, :, :], mk[:, 0, :, :], ALU.mult))
                link(v.tensor_tensor(t2[:, :, :], slots[:, :, :], mk[:, 1, :, :], ALU.mult))
                v.tensor_reduce(slotf[:, 0, tiles(g)], t1[:, :, :], AX.X, ALU.add)
                link(v.tensor_reduce(slotf[:, 1, tiles(g)], t2[:, :, :], AX.X, ALU.add))
                v.tensor_copy(sloti[:, :, tiles(g)], slotf[:, :, tiles(g)]).then_inc(s_slot, 1)

            def row_modulation():
                dve.wait_ge(s_modb, 1)
                for b in range(B):
                    m = bank[4 + b]
                    v.tensor_copy(sbB[:, b, :], m[:, 0:D])
                    v.tensor_scalar(cbB[:, b, :], m[:, D:2 * D], 1.0, None, ALU.add)
                    v.tensor_scalar(gbS[:, b, :], m[:, 2 * D:3 * D], 0.0, 2.0, ALU.is_ge, ALU.mult)
                    link(v.tensor_copy(gbB[:, b, :], m[:, 2 * D:3 * D]))
                link(v.scalar_tensor_tensor(gbB[:, :, :], gbB[:, :, :], -1.0, gbB[:, :, :], ALU.mult, ALU.max))
                link(v.tensor_scalar(gbB[:, :, :], gbB[:, :, :], GATE_FLOOR, None, ALU.max))
                v.scalar_tensor_tensor(gbB[:, :, :], gbS[:, :, :], -1.0, gbB[:, :, :],
                                       ALU.add, ALU.mult).then_inc(s_modok, 1)

            def split_biases():
                dve.wait_ge(s_bin, 32)
                for src, r, p in ((b1_in, b1_r, b1_p), (b2_in, b2_r, b2_p)):
                    link(v.tensor_copy(p[:, 0, :], src[:, :]))
                    link(v.tensor_tensor(r[:, 0, :], src[:, :], p[:, 0, :], ALU.subtract))
                    link(v.tensor_copy(p[:, 1, :], r[:, 0, :]))
                    link(v.tensor_tensor(r[:, 1, :], r[:, 0, :], p[:, 1, :], ALU.subtract))
                    ins = v.tensor_copy(p[:, 2, :], r[:, 1, :])
                ins.then_inc(s_bp, 1)

            def constants():
                dve.wait_ge(s_const, 11)
                v.tensor_copy(eid[:, :, :], iota_i[:, 0:GT * NE].rearrange("p (j e) -> p j e", e=NE))
                v.tensor_copy(k128[:, :], iota_i[0:1, 64:64 + KT])
                v.tensor_copy(tauf[:, :], iota_i[0:1, 128:128 + TILES])
                v.memset(mcum[:, 0, :], 0.0)
                v.memset(mcum_b[:, 0, :], 0.0)
                link(v.memset(one8[:, :], 1.0))
                v.tensor_scalar(eid8[:, :, :], eid[:, :, :], float(NE), None, ALU.add)
                link(v.tensor_scalar(ereg[:, :, :], eid[:, :, :], float(REG), None, ALU.mult))

            ln1_stats(2)
            ln1_stats(3)
            ln1_norm(2)
            row_modulation()
            inputs_u(0)
            ln1_norm(3)
            inputs_u(1)
            ln1_stats(4)
            ln1_norm(4)
            inputs_u(2)
            ln1_stats(5)
            ln1_norm(5)
            inputs_u(3)
            split_biases()
            constants()
            for g in range(GPB):
                if g < 2:
                    ln1_stats(6 + g)
                    ln1_norm(6 + g)
                scan(g)
                inputs_u(GPB + g)
            for g in range(NG + 2):
                if g < NG:
                    residual(g)
                    stats(st2, mv2, ve2, g, s_var2)
                if g < NG - GPB:
                    scan(GPB + g)
                if g < NG:
                    ln2_norm(g)
                if g >= 2:
                    top2(g - 2)

            dve.wait_ge(s_cnt, 1)
            link(v.tensor_copy(cf[:, :], bank[7][0:1, 0:NE]))
            link(v.tensor_tensor(cmpk[:, :, :], cf[:, :].unsqueeze(2).to_broadcast([1, NE, KT]),
                                 k128[:, :].unsqueeze(1).to_broadcast([1, NE, KT]), ALU.is_gt))
            link(v.tensor_reduce(te[:, :], cmpk[:, :, :], AX.X, ALU.add))
            link(v.tensor_tensor_scan(sinc[:, :], one8[:, :], te[:, :], 0.0, ALU.mult, ALU.add))
            link(v.tensor_tensor(cmpt[:, :, :], tauf[:, :].unsqueeze(2).to_broadcast([1, TILES, NE]),
                                 sinc[:, :].unsqueeze(1).to_broadcast([1, TILES, NE]), ALU.is_ge))
            link(v.tensor_tensor(cmpu[:, :, :], cmpt[:, :, :],
                                 te[:, :].unsqueeze(1).to_broadcast([1, TILES, NE]), ALU.mult))
            link(v.tensor_reduce(tf[:, 0, :], cmpt[:, :, :], AX.X, ALU.add))
            link(v.tensor_reduce(tf[:, 1, :], cmpu[:, :, :], AX.X, ALU.add))
            link(v.tensor_tensor(tf[:, 2, :], tauf[:, :], tf[:, 1, :], ALU.subtract))
            link(v.tensor_scalar(tf[:, 3, :], tf[:, 0, :], float(REG), None, ALU.mult))
            link(v.scalar_tensor_tensor(tf[:, 4, :], tf[:, 2, :], float(P), tf[:, 3, :], ALU.mult, ALU.add))
            v.tensor_scalar(tab_row[:, :], tf[:, 4, :], float(NE * REG), None, ALU.min)
            v.tensor_scalar(tab_e[:, :], tf[:, 0, :], float(NE - 1), None, ALU.min)
            link(v.tensor_tensor(pad_f[:, :], cf[:, :], ereg[0:1, 0, :], ALU.add))
            v.tensor_copy(pad_i[:, :], pad_f[:, :]).then_inc(s_tab, 1)

            def copy_x(s, u):
                dve.wait_ge(s_txp, s + 1)
                if not (isinstance(s, int) and s < 2):
                    dve.wait_ge(s_l1, s - 1)
                v.tensor_copy(xT[:, u % 2, :], bank[u % 2][:, 0:P]).then_inc(s_xT, 1)

            def copy_h(s, u):
                dve.wait_ge(s_thp, s + 1)
                if not (isinstance(s, int) and s < 2):
                    dve.wait_ge(s_l2, s - 1)
                v.tensor_copy(hsT[:, u % 2, :, :],
                              bank[4 + u % 2][:, :].rearrange("p (c t) -> p c t", c=HC)).then_inc(s_hsT, 1)

            def scale_y(s, u):
                dve.wait_ge(s_l2, s + 1)
                if not (isinstance(s, int) and s < 4):
                    dve.wait_ge(s_sc[(u - 4) % U], 16 * rounds(s - 4))
                v.tensor_scalar(yo[:, u % 4, :], bank[6 + u % 2][:, 0:D], xr[:, u, D:D + 1], None,
                                ALU.mult).then_inc(s_yo, 1)

            copy_x(0, 0)

            def step(s, u):
                static = isinstance(s, int)
                if not static or s + 1 < TILES:
                    copy_x(s + 1, (u + 1) % U)
                if not static or 1 <= s <= TILES:
                    copy_h(s - 1, (u - 1) % U)
                if not static or s >= 2:
                    scale_y(s - 2, (u - 2) % U)

            expert_steps_skewed(dve, step)

            for g in range(NG):
                b = g // GPB
                dve.wait_ge(s_y01[g % 2], 32 * (g // 2 + 1))
                if g >= 2:
                    dve.wait_ge(s_out[g % 2], 16 * (g // 2))
                f0 = fo[:, g % 2, 0, :, :]
                link(v.tensor_tensor(f0, y01[:, g % 2, 0, :, :], y01[:, g % 2, 1, :, :], ALU.add))
                link(v.tensor_tensor(f0, f0, gbB[:, b, :].unsqueeze(1).to_broadcast([P, GT, D]), ALU.mult))
                v.tensor_tensor(fo[:, g % 2, 1, :, :], f0, xs[:, tiles(g), :], ALU.add).then_inc(s_fin, 1)

        @block.tensor
        def _(pe):
            t = nc.tensor

            def transpose_group(dst, src):
                for j in range(GT):
                    ins = t.transpose(dst[:, j * P:(j + 1) * P], src(j), ident[:, :])
                return ins

            pe.wait_ge(s_cs, 1)
            pe.wait_ge(s_wsm, 48)
            for i in range(6):
                ins = t.matmul(bank[6][:, i * B:(i + 1) * B], wmod_s[:, i * D:(i + 1) * D], csil[:, 0, :],
                               start=True, stop=True)
            ins.then_inc(s_modc, 1)
            for b in range(B):
                ins = t.matmul(bank[4 + b][:, 0:3 * D], csil_b[:, b, :], wmod_s[:, 3 * D:6 * D],
                               start=True, stop=True)
            ins.then_inc(s_modb, 1)

            def xn_transpose(g):
                pe.wait_ge(s_xn, g + 1)
                if g == 0:
                    pe.wait_ge(s_const, 3)
                if g >= 2:
                    pe.wait_ge(s_hT, g - 1)
                transpose_group(bank[g % 2], lambda j: xn[:, g % 2, j, :]).then_inc(s_xnT, 1)

            def gate_products(g):
                if g == 0:
                    pe.wait_ge(s_wbd, 16 * 2 * NH)
                pe.wait_ge(s_hT, g + 1)
                if g >= 1:
                    pe.wait_ge(s_ta, g)
                t.matmul(bank[2][:, :], wx_bd[:, :], hT[:, cols(g)], start=True, stop=True)
                t.matmul(bank[3][:, :], wa_bd[:, :], hT[:, cols(g)], start=True, stop=True).then_inc(s_z, 1)

            def y_transpose(g):
                pe.wait_ge(s_y, g + 1)
                if g == 0:
                    pe.wait_ge(s_modok, 3)
                if g >= 2:
                    pe.wait_ge(s_var2, g - 1)
                transpose_group(bank[4 + g % 2],
                                lambda j: yv[:, g * G + j * P:g * G + (j + 1) * P]).then_inc(s_yT, 1)

            def h2_transpose(g):
                pe.wait_ge(s_h2, g + 1)
                if g == 0:
                    pe.wait_ge(s_hT, NG)
                if g >= 2:
                    pe.wait_ge(s_h2T, g - 1)
                transpose_group(bank[g % 2], lambda j: rows[:, g * GT + j, 0, 0:D]).then_inc(s_h2t, 1)

            def router(g):
                if g == 0:
                    pe.wait_ge(s_rw, 64)
                    pe.wait_ge(s_ta, NG)
                pe.wait_ge(s_h2T, g + 1)
                for h in range(HC):
                    n = HC * g + h
                    if n >= 2:
                        pe.wait_ge(s_hr, n - 1)
                    t.matmul(bank[2 + h % 2][:, :], rw1_s[:, h * P:(h + 1) * P], h2T[:, g % 2, :],
                             start=True, stop=True).then_inc(s_rl1, 1)

            def logits(g):
                pe.wait_ge(s_hr, HC * (g + 1))
                if g == 0:
                    pe.wait_ge(s_modok, 1)
                    pe.wait_ge(s_const, 6)
                if g >= 1:
                    pe.wait_ge(s_lgc, g)
                for j in range(GT):
                    o = bank[6][:, j * NE:(j + 1) * NE]
                    for h in range(HC):
                        t.matmul(o, hr[g % 2][:, h, j * P:(j + 1) * P], rw2_s[:, h, :], start=(h == 0), stop=False)
                    ins = t.matmul(o, ones_row[:, :], rb2_s[:, :], start=False, stop=True)
                ins.then_inc(s_lg, 1)

            def positions(g):
                pe.wait_ge(s_mask, g + 1)
                if g >= 1:
                    pe.wait_ge(s_slot, g)
                for j in range(GT):
                    o = bank[7][:, j * NE:(j + 1) * NE]
                    t.matmul(o, ones_bf[:, :], mcum_b[:, g, :], start=True, stop=False)
                    for i in range(j):
                        t.matmul(o, ones_bf[:, :], mboth[:, g * GT + i, :], start=False, stop=False)
                    ins = t.matmul(o, before[:, :], mboth[:, g * GT + j, :], start=False, stop=True)
                ins.then_inc(s_pos, 1)

            xn_transpose(0)
            xn_transpose(1)
            for g in range(NG):
                gate_products(g)
                if g + 2 < NG:
                    xn_transpose(g + 2)
            for g in range(NG + 2):
                if g < NG:
                    y_transpose(g)
                    h2_transpose(g)
                if 1 <= g <= NG:
                    router(g - 1)
                    logits(g - 1)
                if g >= 2:
                    positions(g - 2)
            pe.wait_ge(s_slot, NG)
            t.matmul(bank[7][:, 0:NE], ones_bf[:, :], mcum_b[:, NG, :], start=True, stop=True).then_inc(s_cnt, 1)

            pe.wait_ge(s_w1, 16 * NE)
            pe.wait_ge(s_w2, 16 * NE)
            pe.wait_ge(s_bs, 16 * 6)
            pe.wait_ge(s_tab, 1)

            def turn_x(s, u):
                pe.wait_ge(s_xr[u], 16 * rounds(s))
                if not (isinstance(s, int) and s < 2):
                    pe.wait_ge(s_xT, s - 1)
                t.transpose(bank[u % 2][:, 0:P], xr[:, u, 0:D], ident[:, :]).then_inc(s_txp, 1)

            def layer1(s, u, e):
                pe.wait_ge(s_xT, s + 1)
                if not (isinstance(s, int) and s < 2):
                    pe.wait_ge(s_hs, s - 1)
                t.matmul(bank[2 + u % 2][:, :], xT[:, u % 2, :], w1_s[:, bass.ds(e * HID, HID)],
                         start=True, stop=False)
                t.matmul(bank[2 + u % 2][:, :], ones_bf[0:3, :], b1_s[:, bass.ds(e * HID, HID)],
                         start=False, stop=True).then_inc(s_l1, 1)

            def turn_h(s, u):
                pe.wait_ge(s_hs, s + 1)
                if not (isinstance(s, int) and s < 2):
                    pe.wait_ge(s_hsT, s - 1)
                for h in range(HC):
                    ins = t.transpose(bank[4 + u % 2][:, h * P:(h + 1) * P], hs[:, u % 2, h * P:(h + 1) * P],
                                      ident[:, :])
                ins.then_inc(s_thp, 1)

            def layer2(s, u, e):
                pe.wait_ge(s_hsT, s + 1)
                if not (isinstance(s, int) and s < 2):
                    pe.wait_ge(s_yo, s - 1)
                o = bank[6 + u % 2][:, 0:D]
                for h in range(HC):
                    t.matmul(o, hsT[:, u % 2, h, :], w2_s[:, bass.ds(e * (HC * D) + h * D, D)],
                             start=(h == 0), stop=False)
                t.matmul(o, ones_bf[0:3, :], b2_s[:, bass.ds(e * D, D)], start=False, stop=True).then_inc(s_l2, 1)

            def expert_of(s):
                return pe.value_load(tab_e[0:1, bass.ds(s, 1)], min_val=0, max_val=NE - 1)

            turn_x(0, 0)

            def step(s, u):
                static = isinstance(s, int)
                if not static or s + 1 < TILES:
                    turn_x(s + 1, (u + 1) % U)
                if not static or s < TILES:
                    layer1(s, u, expert_of(s))
                if not static or 1 <= s <= TILES:
                    turn_h(s - 1, (u - 1) % U)
                if not static or s >= 2:
                    layer2(s - 2, (u - 2) % U, expert_of(s - 2))

            expert_steps_skewed(pe, step)


_INS = ['L0_attn_x', 'L0_attn_a_param', 'L0_attn_w_in', 'L0_attn_w_a', 'L0_ffn_rw1', 'L0_ffn_rb1', 'L0_ffn_rw2',
        'L0_ffn_rb2', 'L0_ffn_w1', 'L0_ffn_b1', 'L0_ffn_w2', 'L0_ffn_b2', 'L0_c', 'L0_wmod']
_OUTS = [((2, 2048, 128), 'float32')]


def kernel(**inputs):
    import numpy as _np
    import concourse.bacc as _bacc
    from concourse import mybir as _mybir
    from concourse.bass_utils import run_bass_kernel_spmd as _run

    nc = _bacc.Bacc("TRN2", target_bir_lowering=False, num_devices=1)
    arrays, args = {}, []
    for name in _INS:
        a = _np.ascontiguousarray(inputs[name])
        arrays[f"in_{name}_dram"] = a
        args.append(nc.dram_tensor(f"in_{name}_dram", a.shape, _mybir.dt.from_np(a.dtype), kind="ExternalInput").ap())
    for i, (shape, dtype) in enumerate(_OUTS):
        dt = _mybir.dt.from_np(_np.dtype(dtype))
        args.append(nc.dram_tensor(f"out_{i}_dram", shape, dt, kind="ExternalOutput").ap())
    adaln_block(nc, *args)
    r = _run(nc, [arrays], core_ids=[0])
    got = tuple(r.results[0][f"out_{i}_dram"] for i in range(len(_OUTS)))
    return got[0]
```

```python
from contextlib import ExitStack

import concourse.bass as bass
from concourse import mybir

ALU = mybir.AluOpType
ACT = mybir.ActivationFunctionType
AX = mybir.AxisListType
F32 = mybir.dt.float32
BF16 = mybir.dt.bfloat16
I32 = mybir.dt.int32

P = 128
EPS = 1e-5
GATE_FLOOR = 0.25
NEG_HUGE = -3.0e38
EULER = 2.718281828459045


def adaln_block(nc, x, a_param, w_in, w_a, rw1, rb1, rw2, rb2, w1, b1, w2, b2, c, wmod, out):
    B, T, D = x.shape
    NH, HB, _ = w_in.shape
    HID = rw1.shape[1]
    NE = rw2.shape[1]
    TOK = B * T
    NT = TOK // P
    GT = 4
    G = GT * P
    NG = TOK // G
    GPB = NG // B
    HC = HID // P
    TOPK = 2
    HALVES = 2
    SL = HALVES * P
    REG = TOK + SL
    ROW = D + 2
    WE = HID + HC
    U = 4
    TILES = (TOPK * TOK + NE * (SL - 1)) // SL
    KT = TOK // SL
    RG = 2
    RB = RG * GT
    NR = NG // RG
    assert D == P and HC == GT and B == 2 and NG == 8 and TILES >= 3 * U

    x_t = x.rearrange("b (n p) d -> p (b n) d", p=P)
    out_t = out.rearrange("b (n p) d -> p (b n) d", p=P)

    with ExitStack() as ctx:
        def sb(name, shape, dt=F32):
            return ctx.enter_context(nc.sbuf_tensor(name, shape, dt))

        def ps(name, shape, dt=F32):
            return ctx.enter_context(nc.psum_tensor(name, shape, dt))

        def sem(name):
            return ctx.enter_context(nc.semaphore(name))

        sorted_rows = nc.dram_tensor("sorted_rows", [NE * REG + SL, ROW], F32)
        expert_out = nc.dram_tensor("expert_out", [TOPK * TOK, D], F32)

        xs = sb("xs", [P, NT, D])
        wx_bd = sb("wx_bd", [P, P])
        wa_bd = sb("wa_bd", [P, P])
        rw1_s = sb("rw1_s", [P, HID])
        rw2_s = sb("rw2_s", [P, HC, NE])
        rb2_s = sb("rb2_s", [1, NE])
        w1_s = sb("w1_s", [P, NE * WE])
        w2_s = sb("w2_s", [P, NE * HC * D])
        wmod_s = sb("wmod_s", [P, 6 * D])
        NSM = B + 1 + HC + NE * HC
        small = sb("small", [NSM, P])
        smallT = sb("smallT", [P, NSM])
        cT = smallT[:, 0:B]
        apar = smallT[:, B:B + 1]
        rb1_s = smallT[:, B + 1:B + 1 + HC]
        b1_c = smallT[:, B + 1 + HC:NSM].rearrange("p (e h) -> p e h", h=HC)
        wx_c = sb("wx_c", [P, HB])
        wa_c = sb("wa_c", [P, HB])
        csil = sb("csil", [P, 3, B])
        csil_b = sb("csil_b", [P, B, P])
        softp = sb("softp", [P, 8])
        modc = sb("modc", [P, 6, B])
        gac = sb("gac", [P, 3, B])
        sbB = sb("sbB", [P, B, D])
        cbB = sb("cbB", [P, B, D])
        gbB = sb("gbB", [P, B, D])
        gbS = sb("gbS", [P, B, D])
        ident = sb("ident", [P, P])
        before = sb("before", [P, P], BF16)
        ones_bf = sb("ones_bf", [P, P], BF16)
        ones_row = sb("ones_row", [1, P])
        half_neg = sb("half_neg", [P, GT])
        euler = sb("euler", [P, RB])
        b2_in = sb("b2_in", [P, NE * D // P])
        b2_r = sb("b2_r", [P, 2, NE * D // P])
        b2_p = sb("b2_p", [P, 3, NE * D // P], BF16)
        b2_s = sb("b2_s", [3, NE * D], BF16)
        st1 = sb("st1", [P, NT, 6])
        mv1 = sb("mv1", [P, NT, 2])
        ve1 = sb("ve1", [P, NT])
        rs1 = sb("rs1", [P, NT])
        st2 = sb("st2", [P, NT, 6])
        mv2 = sb("mv2", [P, NT, 2])
        ve2 = sb("ve2", [P, NT])
        rs2 = sb("rs2", [P, NT])
        xn = sb("xn", [P, 2, GT, D])
        hT = sb("hT", [P, TOK])
        tx = sb("tx", [P, TOK])
        ta = sb("ta", [P, 2, G])
        av = sb("av", [P, TOK])
        qv = sb("qv", [P, TOK])
        yv = hT
        rows = sb("rows", [P, NT, TOPK, ROW])
        h2T = sb("h2T", [P, 2, G])
        hr = [z[:, 0:HC * G].rearrange("p (h t) -> p h t", h=HC) for z in (av, qv)]
        iota_i = sb("iota_i", [P, 256], I32)
        eid = sb("eid", [P, RB, NE])
        eid8 = sb("eid8", [P, RB, NE])
        ereg = sb("ereg", [P, RB, NE])
        lg = sb("lg", [P, RB, NE])
        t1 = sb("t1", [P, RB, NE])
        t2 = sb("t2", [P, RB, NE])
        mk = sb("mk", [P, TOPK, RB, NE])
        best = sb("best", [P, TOPK, RB])
        bidx = sb("bidx", [P, TOPK, RB])
        mboth = sb("mboth", [P, NT, NE], BF16)
        mcum = sb("mcum", [P, NR + 1, NE])
        mcum_b = sb("mcum_b", [P, NR + 1, NE], BF16)
        msum = sb("msum", [P, NE])
        dlt = sb("dlt", [P, 2, RB])
        edl = sb("edl", [P, 2, RB])
        prb = sb("prb", [P, 2, RB])
        slots = sb("slots", [P, RB, NE])
        slotf = sb("slotf", [P, TOPK, NT])
        sloti = sb("sloti", [P, TOPK, NT], I32)
        padr = sb("padr", [P, HALVES, ROW])
        cf = sb("cf", [1, NE])
        kslots = sb("kslots", [1, KT])
        tauf = sb("tauf", [1, TILES])
        cmpk = sb("cmpk", [1, NE, KT])
        te = sb("te", [1, NE])
        sinc = sb("sinc", [1, NE])
        one8 = sb("one8", [1, NE])
        cmpt = sb("cmpt", [1, TILES, NE])
        cmpu = sb("cmpu", [1, TILES, NE])
        tf = sb("tf", [1, 5, TILES])
        tab_row = sb("tab_row", [1, TILES], I32)
        tab_e = sb("tab_e", [1, TILES], I32)
        pad_f = sb("pad_f", [1, NE])
        pad_i = sb("pad_i", [1, NE], I32)
        spare = [0]

        def in_tx(n):
            spare[0] += n
            assert spare[0] <= TOK
            return tx[:, spare[0] - n:spare[0]]

        xr = in_tx(U * HALVES * ROW).rearrange("p (u n r) -> p u n r", u=U, n=HALVES)
        hsT = in_tx(2 * HC * SL).rearrange("p (r h t) -> p r h t", r=2, h=HC)
        yo = in_tx(2 * HALVES * D).rearrange("p (r n d) -> p r n d", r=2, n=HALVES)
        xT = h2T[:, :, 0:SL]
        prob_t = sb("prob_t", [P, U, HALVES, 1])
        dest_t = sb("dest_t", [P, U, HALVES, 1], I32)
        w1_t = sb("w1_t", [P, 2, WE])
        y01 = [z[:, i * TOPK * G:(i + 1) * TOPK * G].rearrange("p (k n d) -> p k n d", k=TOPK, d=D)
               for z in (av, qv) for i in range(NG // 2)]

        bank = [ps(f"bank{i}", [P, 512]) for i in range(8)]

        def sems(*names):
            return [sem(n) for n in names]

        s_x = sems(*(f"s_x{g}" for g in range(NG)))
        s_small, s_wmod, s_wc, s_rw, s_w1, s_w2, s_b2in, s_b2s = sems(
            "s_small", "s_wmod", "s_wc", "s_rw", "s_w1", "s_w2", "s_b2in", "s_b2s")
        s_zero, s_ident, s_const, s_wsel, s_wbd, s_turned, s_cols, s_absa, s_ecs, s_esp, s_cs = sems(
            "s_zero", "s_ident", "s_const", "s_wsel", "s_wbd", "s_turned", "s_cols", "s_absa", "s_ecs",
            "s_esp", "s_cs")
        s_modc, s_modb, s_modok, s_softp, s_modrow, s_b2p, s_dve = sems(
            "s_modc", "s_modb", "s_modok", "s_softp", "s_modrow", "s_b2p", "s_dve")
        s_var1, s_rstd1, s_xn, s_xnT, s_hT, s_z, s_ta, s_exp, s_u, s_m, s_y, s_yT = sems(
            "s_var1", "s_rstd1", "s_xn", "s_xnT", "s_hT", "s_z", "s_ta", "s_exp", "s_u", "s_m", "s_y", "s_yT")
        s_res, s_var2, s_rstd2, s_h2, s_h2t, s_h2T, s_dup, s_rl1, s_hr, s_lg, s_lgc, s_mask, s_pos = sems(
            "s_res", "s_var2", "s_rstd2", "s_h2", "s_h2t", "s_h2T", "s_dup", "s_rl1", "s_hr", "s_lg", "s_lgc",
            "s_mask", "s_pos")
        s_dlt, s_edl, s_slot, s_disp, s_cnt, s_tab, s_pad = sems(
            "s_dlt", "s_edl", "s_slot", "s_disp", "s_cnt", "s_tab", "s_pad")
        s_xr = sems(*(f"s_xr{i}" for i in range(U)))
        s_txp, s_xT, s_w1t, s_l1, s_hs, s_l2, s_yo, s_fin = sems(
            "s_txp", "s_xT", "s_w1t", "s_l1", "s_hs", "s_l2", "s_yo", "s_fin")
        s_taken, s_out = sems("s_taken", "s_out")
        s_sc = sems(*(f"s_sc{i}" for i in range(U)))
        s_y01 = sems(*(f"s_y01_{g}" for g in range(NG)))

        rows_i = rows[:, :, :, :].bitcast(I32)
        padr_i = padr[:, :, :].bitcast(I32)
        xr_i = xr.bitcast(I32)
        block = ctx.enter_context(nc.Block())

        def cols(g):
            return slice(g * G, (g + 1) * G)

        def tiles(g):
            return slice(g * GT, (g + 1) * GT)

        def blk(r):
            return slice(r * RB, (r + 1) * RB)

        PLAN = [stage.split(":") for stage in """
            ln1s:0 ln1s:1 setup:0 ln1n:0 ln1n:1 mod:0 ln1s:2 mod:1 gate:0 ln1n:2 ln1s:3 mod:2 gate:1 ln1n:3 mod:3
            gate:2 gate:3 late:0 mult:0 mult:1 mult:2 mult:3
            scan:0 scan:1 ln2s:0 scan:2 ln2s:1 scan:3 ln2s:2 ln2n:0 rout:0 ln2s:3 ln2n:1 ln1s:4 ln1s:5 logi:0
            rout:1 ln2n:2 ln1n:4 ln1s:6 ln1n:5 logi:1 ln2n:3 ln1s:7 top:0 mod:4 mod:5 pos:0 disp:0 disp:1
            gate:4 ln1n:6 mod:6 gate:5 ln1n:7 mod:7 gate:6 gate:7 mult:4 mult:5 mult:6 mult:7
            rout:2 scan:4 scan:5 logi:2 ln2s:4 scan:6 rout:3 ln2s:5 scan:7 logi:3 ln2s:6 ln2n:4 top:1 ln2s:7
            ln2n:5 rout:4 pos:1 disp:2 logi:4 rout:5 disp:3 ln2n:6 logi:5 ln2n:7 top:2 rout:6 pos:2 disp:4
            disp:5 logi:6 rout:7 logi:7 top:3 pos:3 disp:6 disp:7""".split()]
        PLAN = [(name, int(n)) for name, n in PLAN]

        def run(stages):
            for name, n in PLAN:
                if name in stages:
                    stages[name](n)

        TURNS = [(name, g) for name, g in PLAN if name in ("ln1n", "scan", "ln2n")]
        READ = {"ln1n": s_hT, "scan": s_res, "ln2n": s_h2T}

        READER = {"ln1n": "ln1n", "scan": "ln2s", "ln2n": "ln2n"}
        for (name, g), later in zip(TURNS, TURNS[2:]):
            assert PLAN.index((READER[name], g)) < PLAN.index(later), (name, g, later)

        def turn_bank(name, g):
            return bank[TURNS.index((name, g)) % 2]

        def wait_turn_bank(pe, name, g):
            n = TURNS.index((name, g))
            if n >= 2:
                before_name, before_g = TURNS[n - 2]
                pe.wait_ge(READ[before_name], before_g + 1)

        LOOPS = (TILES - 3) // U

        def expert_steps(eng, body, last):
            for s in range(U):
                body(s, s)
            with eng.Fori(1, LOOPS) as n:
                for u in range(U):
                    body(n * U + u, u)
            for s in range(LOOPS * U, last):
                body(s, s % U)

        def static(s):
            return isinstance(s, int)

        def rounds(s, u):
            return (s - u) // U + 1

        @block.sync
        def _(sp):
            sp.dma_start(xs[:, tiles(0), :], x_t[:, tiles(0), :]).then_inc(s_x[0], 16)
            sp.dma_start(wmod_s[:, :], wmod).then_inc(s_wmod, 16)
            for g in range(1, GPB):
                sp.dma_start(xs[:, tiles(g), :], x_t[:, tiles(g), :]).then_inc(s_x[g], 16)
            sp.dma_start(rw1_s[:, :], rw1).then_inc(s_rw, 16)
            sp.dma_start(rw2_s[:, :, :], rw2.rearrange("(c p) e -> p c e", p=P)).then_inc(s_rw, 16)
            sp.dma_start(rb2_s[:, :], rb2.rearrange("(a e) -> a e", a=1)).then_inc(s_rw, 16)
            sp.dma_start(b2_in[:, :], b2.rearrange("e (q n) -> (e q) n", q=P // NE)).then_inc(s_b2in, 16)
            for g in range(GPB, NG):
                sp.dma_start(xs[:, tiles(g), :], x_t[:, tiles(g), :]).then_inc(s_x[g], 16)
            for e in range(NE):
                sp.dma_start(w1_s[:, e * WE:e * WE + HID], w1[e]).then_inc(s_w1, 16)
                sp.dma_start(w2_s[:, e * HC * D:(e + 1) * HC * D].rearrange("p (c d) -> p c d", c=HC),
                             w2[e].rearrange("(c p) d -> p c d", p=P)).then_inc(s_w2, 16)
            sp.wait_ge(s_b2p, 1)
            for k in range(3):
                sp.dma_start(b2_s[k:k + 1, :], b2_p[:, k, :]).then_inc(s_b2s, 16)

            def padding(row):
                sp.dma_start(sorted_rows[row, :].rearrange("(n p) r -> p n r", p=P),
                             padr[:, :, :]).then_inc(s_pad, 16)

            sp.wait_ge(s_const, 8)
            padding(slice(NE * REG, NE * REG + SL))
            sp.wait_ge(s_tab, 1)
            for e in range(NE):
                padding(bass.ds(sp.value_load(pad_i[0:1, e:e + 1], min_val=e * REG, max_val=e * REG + TOK), SL))
            sp.wait_ge(s_pad, 16 * (NE + 1))
            sp.wait_ge(s_disp, 16 * TOPK * NT)

            def load(s, u):
                r = sp.value_load(tab_row[0:1, bass.ds(s, 1)], min_val=0, max_val=NE * REG)
                if not (static(s) and s < U):
                    sp.wait_ge(s_taken, s - U + 1)
                sp.dma_start(xr[:, u, :, :], sorted_rows[bass.ds(r, SL), :]
                             .rearrange("(n p) r -> p n r", p=P)).then_inc(s_xr[u], 16)

            expert_steps(sp, load, TILES)
            for u in range(U):
                sp.wait_ge(s_sc[u], 16 * HALVES * ((TILES - 1 - u) // U + 1))
            for g in range(NG):
                for k in range(TOPK):
                    sp.dma_start(y01[g][:, k, :, :],
                                 expert_out[k * TOK + g * G:k * TOK + (g + 1) * G, :]
                                 .rearrange("(n p) d -> p n d", p=P)).then_inc(s_y01[g], 16)

        @block.gpsimd
        def _(pool):
            p = nc.gpsimd
            p.memset(ident[:, :], 0.0).then_inc(s_zero, 1)
            p.memset(half_neg[:, :], -0.5).then_inc(s_const, 1)
            pool.wait_ge(s_zero, 1)
            p.affine_select(out=ident[:, :], in_=ident[:, :], compare_op=ALU.not_equal, fill=1.0,
                            base=0, pattern=[[-1, P]], channel_multiplier=1).then_inc(s_ident, 1)
            pool.wait_ge(s_wc, 32)
            for w_c, w_bd in ((wx_c, wx_bd), (wa_c, wa_bd)):
                blocks = w_bd[:, :].rearrange("p (h e) -> p h e", h=NH)
                ins = p.affine_select(out=blocks, in_=w_c[:, :].unsqueeze(1).to_broadcast([P, NH, HB]),
                                      compare_op=ALU.is_ge, fill=0.0, base=0, pattern=[[-HB, NH], [0, HB]],
                                      channel_multiplier=1)
            ins.then_inc(s_wsel, 1)
            pool.wait_ge(s_wsel, 1)
            for w_bd in (wx_bd, wa_bd):
                blocks = w_bd[:, :].rearrange("p (h e) -> p h e", h=NH)
                ins = p.affine_select(out=blocks, in_=blocks, compare_op=ALU.is_ge, fill=0.0, base=HB - 1,
                                      pattern=[[HB, NH], [0, HB]], channel_multiplier=-1)
            ins.then_inc(s_wbd, 1)

            def rstd1(g):
                pool.wait_ge(s_var1, g + 1)
                p.tensor_tensor(rs1[:, tiles(g)], ve1[:, tiles(g)], half_neg[:, :], ALU.pow).then_inc(s_rstd1, 1)

            def constants(_):
                p.memset(before[:, :], 1.0).then_inc(s_zero, 1)
                pool.wait_ge(s_zero, 2)
                p.affine_select(out=before[:, :], in_=before[:, :], compare_op=ALU.is_gt, fill=0.0,
                                base=0, pattern=[[1, P]], channel_multiplier=-1).then_inc(s_const, 1)
                p.memset(ones_bf[:, :], 1.0).then_inc(s_const, 1)
                p.memset(ones_row[:, :], 1.0).then_inc(s_const, 1)
                p.memset(euler[:, :], EULER).then_inc(s_const, 1)
                p.iota(iota_i[:, 0:RB * NE], pattern=[[0, RB], [1, NE]], base=0, channel_multiplier=0)
                p.iota(iota_i[0:1, 64:64 + KT], pattern=[[SL, KT]], base=0, channel_multiplier=0)
                p.iota(iota_i[0:1, 128:128 + TILES], pattern=[[1, TILES]], base=0,
                       channel_multiplier=0).then_inc(s_const, 1)
                for k in range(TOPK):
                    ins = p.iota(rows_i[:, :, k, D + 1], pattern=[[P, NT]], base=k * TOK, channel_multiplier=1)
                ins.then_inc(s_const, 1)
                p.memset(padr[:, :, :], 0.0).then_inc(s_zero, 1)
                pool.wait_ge(s_zero, 3)
                p.iota(padr_i[:, :, D + 1], pattern=[[P, HALVES]], base=TOPK * TOK,
                       channel_multiplier=1).then_inc(s_const, 1)

            def rstd2(g):
                pool.wait_ge(s_var2, g + 1)
                p.tensor_tensor(rs2[:, tiles(g)], ve2[:, tiles(g)], half_neg[:, :], ALU.pow).then_inc(s_rstd2, 1)

            def exp_delta(r):
                pool.wait_ge(s_dlt, r + 1)
                p.tensor_tensor(edl[:, r % 2, :], euler[:, :], dlt[:, r % 2, :], ALU.pow).then_inc(s_edl, 1)

            def dispatch(g):
                pool.wait_ge(s_slot, g // RG + 1)
                pool.wait_ge(s_dup, g + 1)
                for t in range(g * GT, (g + 1) * GT):
                    for k in range(TOPK):
                        p.indirect_dma_start(
                            sorted_rows[:, :], bass.IndirectOffsetOnAxis(ap=sloti[:, k, t:t + 1], axis=0),
                            rows[:, t, k, :], None).then_inc(s_disp, 16)

            run({"ln1s": rstd1, "late": constants, "ln2s": rstd2, "top": exp_delta, "disp": dispatch})

            last_row = pool.to_reg(TOPK * TOK - 1)
            for s in range(TILES):
                for n in range(HALVES):
                    pool.wait_ge(s_yo, HALVES * s + n + 1)
                    p.indirect_dma_start(
                        expert_out[:, :], bass.IndirectOffsetOnAxis(ap=dest_t[:, s % U, n, :], axis=0),
                        yo[:, s % 2, n, :], None, bounds_check=last_row, oob_is_err=False).then_inc(s_sc[s % U], 16)

        @block.scalar
        def _(act):
            act.dma_start(small[0:B, :], c).then_inc(s_small, 16)
            act.dma_start(small[B:B + 1, :], a_param.rearrange("(a p) -> a p", a=1)).then_inc(s_small, 16)
            act.dma_start(small[B + 1:B + 1 + HC, :], rb1.rearrange("(h p) -> h p", p=P)).then_inc(s_small, 16)
            act.dma_start(small[B + 1 + HC:NSM, :], b1.rearrange("e (h p) -> (e h) p", p=P)).then_inc(s_small, 16)
            act.dma_start(wx_c[:, :], w_in.rearrange("h d e -> (h d) e")).then_inc(s_wc, 16)
            act.dma_start(wa_c[:, :], w_a.rearrange("h d e -> (h d) e")).then_inc(s_wc, 16)
            act.wait_ge(s_cols, 1)
            nc.scalar.activation(csil[:, 0, :], cT, ACT.Exp, scale=-1.0).then_inc(s_ecs, 1)
            act.wait_ge(s_absa, 1)
            nc.scalar.activation(softp[:, 1:2], softp[:, 0:1], ACT.Exp, scale=-1.0).then_inc(s_esp, 1)

            def modulate(g):
                act.wait_ge(s_xnT, g + 1)
                if g == 0:
                    act.wait_ge(s_modok, 1)
                b = g // GPB
                nc.scalar.activation(hT[:, cols(g)], turn_bank("ln1n", g)[:, :], ACT.Identity,
                                     bias=modc[:, 0, b:b + 1], scale=gac[:, 0, b:b + 1]).then_inc(s_hT, 1)

            def gates(g):
                act.wait_ge(s_z, g + 1)
                nc.scalar.activation(tx[:, cols(g)], bank[2][:, :], ACT.Tanh, scale=0.5)
                nc.scalar.activation(ta[:, g % 2, :], bank[3][:, :], ACT.Tanh, scale=0.5).then_inc(s_ta, 1)

            def decay(g):
                if g == 0:
                    act.wait_ge(s_softp, 1)
                act.wait_ge(s_ta, g + 1)
                nc.scalar.activation(av[:, cols(g)], ta[:, g % 2, :], ACT.Exp, bias=softp[:, 6:7],
                                     scale=softp[:, 6:7])
                nc.scalar.activation(qv[:, cols(g)], ta[:, g % 2, :], ACT.Exp, bias=softp[:, 7:8],
                                     scale=softp[:, 7:8]).then_inc(s_exp, 1)

            def multiplier(g):
                act.wait_ge(s_u, g + 1)
                nc.scalar.activation(qv[:, cols(g)], qv[:, cols(g)], ACT.Sqrt, bias=gac[:, 2, 0:1],
                                     scale=-0.25).then_inc(s_m, 1)

            def router_copy(g):
                act.wait_ge(s_h2t, g + 1)
                if g >= 2:
                    act.wait_ge(s_rl1, HC * (g - 1))
                nc.scalar.copy(h2T[:, g % 2, :], turn_bank("ln2n", g)[:, :]).then_inc(s_h2T, 1)
                nc.scalar.copy(rows[:, tiles(g), 1, 0:D], rows[:, tiles(g), 0, 0:D]).then_inc(s_dup, 1)

            def router_silu(g):
                if g >= 2:
                    act.wait_ge(s_lg, g - 1)
                for h in range(HC):
                    act.wait_ge(s_rl1, HC * g + h + 1)
                    nc.scalar.activation(hr[g % 2][:, h, :], bank[4 + h % 2][:, :], ACT.Silu,
                                         bias=rb1_s[:, h:h + 1]).then_inc(s_hr, 1)

            def gates_and_decay(g):
                gates(g)
                decay(g)

            run({"ln1n": modulate, "gate": gates_and_decay, "mult": multiplier, "ln2n": router_copy,
                 "rout": router_silu})

            def hidden(s, u):
                for q in range(2):
                    act.wait_ge(s_l1, 2 * s + q + 1)
                    if q == 0 and not (static(s) and s < 2):
                        act.wait_ge(s_l2, HALVES * (s - 1))
                    for h in (2 * q, 2 * q + 1):
                        ins = nc.scalar.activation(
                            hsT[:, u % 2, h, :], bank[2 + 2 * (u % 2) + q][:, (h % 2) * SL:(h % 2 + 1) * SL],
                            ACT.Silu, bias=w1_t[:, u % 2, HID + h:HID + h + 1])
                    ins.then_inc(s_hs, 1)

            expert_steps(act, hidden, TILES)

            for g in range(NG):
                act.wait_ge(s_fin, g + 1)
                act.dma_start(out_t[:, tiles(g), :], y01[g][:, 0, :, :]).then_inc(s_out, 16)
            act.wait_ge(s_out, 16 * NG)

        @block.vector
        def _(dve):
            chain = [0]

            def link(ins):
                chain[0] += 1
                ins.then_inc(s_dve, 1)
                dve.wait_ge(s_dve, chain[0])

            v = nc.vector

            def stats(st, mv, ve, g, done):
                for t in range(g * GT, (g + 1) * GT):
                    ins = v.bn_stats(st[:, t, :], xs[:, t, :])
                link(ins)
                for t in range(g * GT, (g + 1) * GT):
                    ins = v.bn_aggr(mv[:, t, :], st[:, t, :])
                link(ins)
                v.tensor_scalar(ve[:, tiles(g)], mv[:, tiles(g), 1], EPS, None, ALU.add).then_inc(done, 1)

            def ln1_stats(g):
                dve.wait_ge(s_x[g], 16)
                stats(st1, mv1, ve1, g, s_var1)

            def ln1_norm(g):
                dve.wait_ge(s_rstd1, g + 1)
                if g >= 2:
                    dve.wait_ge(s_xnT, g - 1)
                for j in range(GT):
                    t = g * GT + j
                    ins = v.tensor_scalar(xn[:, g % 2, j, :], xs[:, t, :], mv1[:, t, 0:1], rs1[:, t:t + 1],
                                          ALU.subtract, ALU.mult)
                ins.then_inc(s_xn, 1)

            def setup(_):
                dve.wait_ge(s_turned, 1)
                v.tensor_copy(smallT[:, :], bank[7][:, 0:NSM]).then_inc(s_cols, 1)
                dve.wait_ge(s_cols, 1)
                v.scalar_tensor_tensor(softp[:, 0:1], apar, -1.0, apar, ALU.mult, ALU.max).then_inc(s_absa, 1)
                dve.wait_ge(s_ecs, 1)
                link(v.tensor_scalar(csil[:, 1, :], csil[:, 0, :], 1.0, None, ALU.add))
                link(v.reciprocal(csil[:, 2, :], csil[:, 1, :]))
                link(v.tensor_tensor(csil[:, 0, :], cT, csil[:, 2, :], ALU.mult))
                v.tensor_copy(csil_b[:, :, :], csil[:, 0, :].unsqueeze(2).to_broadcast([P, B, P])).then_inc(s_cs, 1)
                dve.wait_ge(s_modc, 1)
                link(v.tensor_copy(modc[:, :, :], bank[6][:, 0:6 * B].rearrange("p (i b) -> p i b", b=B)))
                v.memset(gac[:, 2, :], 0.25)
                v.tensor_scalar(gac[:, 0, :], modc[:, 1, :], 1.0, None, ALU.add).then_inc(s_modok, 1)

            def softplus():
                dve.wait_ge(s_esp, 1)
                link(v.tensor_scalar(softp[:, 2:3], softp[:, 1:2], 2.0, None, ALU.add))
                link(v.reciprocal(softp[:, 3:4], softp[:, 2:3]))
                link(v.tensor_tensor(softp[:, 2:3], softp[:, 1:2], softp[:, 3:4], ALU.mult))
                link(v.tensor_tensor(softp[:, 3:4], softp[:, 2:3], softp[:, 2:3], ALU.mult))
                link(v.tensor_scalar(softp[:, 4:5], softp[:, 3:4], 1 / 17, 1 / 15, ALU.mult, ALU.add))
                for k in range(13, 0, -2):
                    link(v.tensor_scalar(softp[:, 4:5], softp[:, 4:5], softp[:, 3:4], 1 / k, ALU.mult, ALU.add))
                link(v.tensor_scalar(softp[:, 5:6], apar, 0.0, 0.5, ALU.max, ALU.mult))
                link(v.tensor_scalar(softp[:, 4:5], softp[:, 4:5], softp[:, 2:3], softp[:, 5:6], ALU.mult, ALU.add))
                v.tensor_scalar(softp[:, 6:7], softp[:, 4:5], -8.0, None, ALU.mult)
                v.tensor_scalar(softp[:, 7:8], softp[:, 4:5], -16.0, None, ALU.mult).then_inc(s_softp, 1)

            def inputs_u(g):
                dve.wait_ge(s_exp, g + 1)
                v.tensor_scalar(qv[:, cols(g)], qv[:, cols(g)], 1.0, None, ALU.min).then_inc(s_u, 1)
                v.scalar_tensor_tensor(tx[:, cols(g)], tx[:, cols(g)], 1.0, hT[:, cols(g)],
                                       ALU.add, ALU.mult)

            def scan(g):
                b = g // GPB
                dve.wait_ge(s_m, g + 1)
                link(v.scalar_tensor_tensor(tx[:, cols(g)], tx[:, cols(g)], gac[:, 1, b:b + 1], qv[:, cols(g)],
                                            ALU.mult, ALU.mult))
                if g % GPB:
                    dve.wait_ge(s_y, g)
                init = 0.0 if g % GPB == 0 else yv[:, g * G - 1:g * G]
                v.tensor_tensor_scan(yv[:, cols(g)], av[:, cols(g)], tx[:, cols(g)], init,
                                     ALU.mult, ALU.add).then_inc(s_y, 1)

            def residual(g):
                dve.wait_ge(s_yT, g + 1)
                v.tensor_tensor(xs[:, tiles(g), :], turn_bank("scan", g)[:, :].rearrange("p (n d) -> p n d", d=D),
                                xs[:, tiles(g), :], ALU.add).then_inc(s_res, 1)
                dve.wait_ge(s_res, g + 1)

            def ln2_norm(g):
                b = g // GPB
                dve.wait_ge(s_rstd2, g + 1)
                for j in range(GT):
                    t = g * GT + j
                    ins = v.scalar_tensor_tensor(rows[:, t, 0, 0:D], xs[:, t, :], mv2[:, t, 0:1], cbB[:, b, :],
                                                 ALU.subtract, ALU.mult)
                link(ins)
                for j in range(GT):
                    t = g * GT + j
                    ins = v.scalar_tensor_tensor(rows[:, t, 0, 0:D], rows[:, t, 0, 0:D], rs2[:, t:t + 1],
                                                 sbB[:, b, :], ALU.mult, ALU.add)
                ins.then_inc(s_h2, 1)

            def top2(r):
                dve.wait_ge(s_lg, RG * (r + 1))
                v.tensor_copy(lg[:, :, :], bank[6][:, 0:RB * NE].rearrange("p (j e) -> p j e", e=NE)).then_inc(s_lgc, 1)
                dve.wait_ge(s_lgc, r + 1)
                for k in range(TOPK):
                    link(v.tensor_reduce(best[:, k, :], lg[:, :, :], AX.X, ALU.max))
                    link(v.tensor_tensor(t1[:, :, :], lg[:, :, :],
                                         best[:, k, :].unsqueeze(2).to_broadcast([P, RB, NE]), ALU.is_ge))
                    link(v.scalar_tensor_tensor(t2[:, :, :], t1[:, :, :], -float(NE), eid8[:, :, :],
                                                ALU.mult, ALU.add))
                    link(v.tensor_reduce(bidx[:, k, :], t2[:, :, :], AX.X, ALU.min))
                    link(v.tensor_tensor(mk[:, k, :, :], eid[:, :, :],
                                         bidx[:, k, :].unsqueeze(2).to_broadcast([P, RB, NE]), ALU.is_equal))
                    if k == 0:
                        link(v.scalar_tensor_tensor(lg[:, :, :], mk[:, 0, :, :], NEG_HUGE, lg[:, :, :],
                                                    ALU.mult, ALU.add))
                v.tensor_tensor(dlt[:, r % 2, :], best[:, 1, :], best[:, 0, :], ALU.subtract).then_inc(s_dlt, 1)
                link(v.tensor_tensor(mboth[:, blk(r), :], mk[:, 0, :, :], mk[:, 1, :, :], ALU.add))
                link(v.tensor_reduce(msum[:, :], mboth[:, blk(r), :].rearrange("p j e -> p e j"), AX.X, ALU.add))
                link(v.tensor_tensor(mcum[:, r + 1, :], mcum[:, r, :], msum[:, :], ALU.add))
                v.tensor_copy(mcum_b[:, r + 1, :], mcum[:, r + 1, :]).then_inc(s_mask, 1)

            def place(r):
                dve.wait_ge(s_edl, r + 1)
                link(v.tensor_scalar(prb[:, 0, :], edl[:, r % 2, :], 1.0, None, ALU.add))
                link(v.reciprocal(prb[:, 1, :], prb[:, 0, :]))
                v.tensor_copy(rows[:, blk(r), 0, D], prb[:, 1, :])
                v.tensor_tensor(rows[:, blk(r), 1, D], edl[:, r % 2, :], prb[:, 1, :], ALU.mult)
                dve.wait_ge(s_pos, r + 1)
                link(v.tensor_tensor(slots[:, :, :], bank[7][:, 0:RB * NE].rearrange("p (j e) -> p j e", e=NE),
                                     ereg[:, :, :], ALU.add))
                v.tensor_tensor(t1[:, :, :], slots[:, :, :], mk[:, 0, :, :], ALU.mult)
                link(v.tensor_tensor(t2[:, :, :], slots[:, :, :], mk[:, 1, :, :], ALU.mult))
                v.tensor_reduce(slotf[:, 0, blk(r)], t1[:, :, :], AX.X, ALU.add)
                link(v.tensor_reduce(slotf[:, 1, blk(r)], t2[:, :, :], AX.X, ALU.add))
                v.tensor_copy(sloti[:, :, blk(r)], slotf[:, :, blk(r)]).then_inc(s_slot, 1)

            def late(_):
                link(v.tensor_scalar(gac[:, 1, :], modc[:, 2, :], 0.0, 2.0, ALU.is_ge, ALU.mult))
                link(v.scalar_tensor_tensor(modc[:, 2, :], modc[:, 2, :], -1.0, modc[:, 2, :], ALU.mult, ALU.max))
                link(v.tensor_scalar(modc[:, 2, :], modc[:, 2, :], GATE_FLOOR, None, ALU.max))
                link(v.scalar_tensor_tensor(gac[:, 1, :], gac[:, 1, :], -1.0, modc[:, 2, :], ALU.add, ALU.mult))
                dve.wait_ge(s_modb, 1)
                for b in range(B):
                    m = bank[4 + b]
                    v.tensor_copy(sbB[:, b, :], m[:, 0:D])
                    v.tensor_scalar(cbB[:, b, :], m[:, D:2 * D], 1.0, None, ALU.add)
                    v.tensor_scalar(gbS[:, b, :], m[:, 2 * D:3 * D], 0.0, 2.0, ALU.is_ge, ALU.mult)
                    ins = v.tensor_copy(gbB[:, b, :], m[:, 2 * D:3 * D])
                ins.then_inc(s_modrow, 1)
                dve.wait_ge(s_modrow, 1)
                link(v.scalar_tensor_tensor(gbB[:, :, :], gbB[:, :, :], -1.0, gbB[:, :, :], ALU.mult, ALU.max))
                link(v.tensor_scalar(gbB[:, :, :], gbB[:, :, :], GATE_FLOOR, None, ALU.max))
                link(v.scalar_tensor_tensor(gbB[:, :, :], gbS[:, :, :], -1.0, gbB[:, :, :], ALU.add, ALU.mult))
                dve.wait_ge(s_b2in, 16)
                link(v.tensor_copy(b2_p[:, 0, :], b2_in[:, :]))
                link(v.tensor_tensor(b2_r[:, 0, :], b2_in[:, :], b2_p[:, 0, :], ALU.subtract))
                link(v.tensor_copy(b2_p[:, 1, :], b2_r[:, 0, :]))
                link(v.tensor_tensor(b2_r[:, 1, :], b2_r[:, 0, :], b2_p[:, 1, :], ALU.subtract))
                v.tensor_copy(b2_p[:, 2, :], b2_r[:, 1, :]).then_inc(s_b2p, 1)
                v.tensor_copy(w1_s[:, :].rearrange("p (e w) -> p e w", e=NE)[:, :, HID:WE], b1_c)
                constants()

            def constants():
                dve.wait_ge(s_const, 6)
                v.tensor_copy(eid[:, :, :], iota_i[:, 0:RB * NE].rearrange("p (j e) -> p j e", e=NE))
                v.tensor_copy(kslots[:, :], iota_i[0:1, 64:64 + KT])
                v.tensor_copy(tauf[:, :], iota_i[0:1, 128:128 + TILES])
                v.memset(mcum[:, 0, :], 0.0)
                v.memset(mcum_b[:, 0, :], 0.0)
                link(v.memset(one8[:, :], 1.0))
                v.tensor_scalar(eid8[:, :, :], eid[:, :, :], float(NE), None, ALU.add)
                link(v.tensor_scalar(ereg[:, :, :], eid[:, :, :], float(REG), None, ALU.mult))

            def gated_inputs(g):
                if g == 0:
                    softplus()
                inputs_u(g)

            def residual_stats(g):
                residual(g)
                stats(st2, mv2, ve2, g, s_var2)

            run({"ln1s": ln1_stats, "setup": setup, "ln1n": ln1_norm, "gate": gated_inputs, "late": late,
                 "scan": scan, "ln2s": residual_stats, "ln2n": ln2_norm, "top": top2, "pos": place})

            dve.wait_ge(s_cnt, 1)
            link(v.tensor_copy(cf[:, :], bank[7][0:1, 0:NE]))
            link(v.tensor_tensor(cmpk[:, :, :], cf[:, :].unsqueeze(2).to_broadcast([1, NE, KT]),
                                 kslots[:, :].unsqueeze(1).to_broadcast([1, NE, KT]), ALU.is_gt))
            link(v.tensor_reduce(te[:, :], cmpk[:, :, :], AX.X, ALU.add))
            link(v.tensor_tensor_scan(sinc[:, :], one8[:, :], te[:, :], 0.0, ALU.mult, ALU.add))
            link(v.tensor_tensor(cmpt[:, :, :], tauf[:, :].unsqueeze(2).to_broadcast([1, TILES, NE]),
                                 sinc[:, :].unsqueeze(1).to_broadcast([1, TILES, NE]), ALU.is_ge))
            link(v.tensor_tensor(cmpu[:, :, :], cmpt[:, :, :],
                                 te[:, :].unsqueeze(1).to_broadcast([1, TILES, NE]), ALU.mult))
            link(v.tensor_reduce(tf[:, 0, :], cmpt[:, :, :], AX.X, ALU.add))
            link(v.tensor_reduce(tf[:, 1, :], cmpu[:, :, :], AX.X, ALU.add))
            link(v.tensor_tensor(tf[:, 2, :], tauf[:, :], tf[:, 1, :], ALU.subtract))
            link(v.tensor_scalar(tf[:, 3, :], tf[:, 0, :], float(REG), None, ALU.mult))
            link(v.scalar_tensor_tensor(tf[:, 4, :], tf[:, 2, :], float(SL), tf[:, 3, :], ALU.mult, ALU.add))
            v.tensor_scalar(tab_row[:, :], tf[:, 4, :], float(NE * REG), None, ALU.min)
            v.tensor_scalar(tab_e[:, :], tf[:, 0, :], float(NE - 1), None, ALU.min)
            link(v.tensor_tensor(pad_f[:, :], cf[:, :], ereg[0:1, 0, :], ALU.add))
            v.tensor_copy(pad_i[:, :], pad_f[:, :]).then_inc(s_tab, 1)

            def prepare(s, u, e):
                dve.wait_ge(s_txp, s + 1)
                if not (static(s) and s < 2):
                    dve.wait_ge(s_l1, 2 * (s - 1))
                    dve.wait_ge(s_hs, 2 * (s - 1))
                v.tensor_copy(xT[:, u % 2, :], bank[u % 2][:, 0:SL]).then_inc(s_xT, 1)
                if not (static(s) and s < U):
                    dve.wait_ge(s_sc[u], 16 * HALVES * (rounds(s, u) - 1))
                v.tensor_copy(prob_t[:, u, :, :], xr[:, u, :, D:D + 1])
                v.tensor_copy(dest_t[:, u, :, :], xr_i[:, u, :, D + 1:D + 2]).then_inc(s_taken, 1)
                v.tensor_copy(w1_t[:, u % 2, :], w1_s[:, bass.ds(e * WE, WE)]).then_inc(s_w1t, 1)

            def scale_y(s, u):
                for n in range(HALVES):
                    dve.wait_ge(s_l2, HALVES * s + n + 1)
                    if n == 0 and not (static(s) and s < 2):
                        dve.wait_ge(s_sc[(u - 2) % U], 16 * HALVES * rounds(s - 2, (u - 2) % U))
                    v.tensor_scalar(yo[:, u % 2, n, :], bank[6 + n][:, 0:D], prob_t[:, u, n, :], None,
                                    ALU.mult).then_inc(s_yo, 1)

            def expert_of(s):
                return dve.value_load(tab_e[0:1, bass.ds(s, 1)], min_val=0, max_val=NE - 1)

            def step(s, u):
                if not static(s) or s + 1 < TILES:
                    prepare(s + 1, (u + 1) % U, expert_of(s + 1))
                if not static(s) or s >= 1:
                    scale_y(s - 1, (u - 1) % U)

            dve.wait_ge(s_w1, 16 * NE)
            dve.wait_ge(s_tab, 1)
            prepare(0, 0, expert_of(0))
            expert_steps(dve, step, TILES + 1)

            for g in range(NG):
                b = g // GPB
                dve.wait_ge(s_y01[g], 16 * TOPK)
                f0 = y01[g][:, 0, :, :]
                link(v.tensor_tensor(f0, f0, y01[g][:, 1, :, :], ALU.add))
                link(v.tensor_tensor(f0, f0, gbB[:, b, :].unsqueeze(1).to_broadcast([P, GT, D]), ALU.mult))
                v.tensor_tensor(f0, f0, xs[:, tiles(g), :], ALU.add).then_inc(s_fin, 1)

        @block.tensor
        def _(pe):
            t = nc.tensor

            def transpose_group(dst, src):
                for j in range(GT):
                    ins = t.transpose(dst[:, j * P:(j + 1) * P], src(j), ident[:, :])
                return ins

            def modulation(_):
                pe.wait_ge(s_ident, 1)
                pe.wait_ge(s_small, 64)
                t.transpose(bank[7][:, 0:NSM], small[:, :], ident[0:NSM, 0:NSM]).then_inc(s_turned, 1)
                pe.wait_ge(s_cs, 1)
                pe.wait_ge(s_wmod, 16)
                for i in range(6):
                    ins = t.matmul(bank[6][:, i * B:(i + 1) * B], wmod_s[:, i * D:(i + 1) * D], csil[:, 0, :],
                                   start=True, stop=True)
                ins.then_inc(s_modc, 1)
                for b in range(B):
                    ins = t.matmul(bank[4 + b][:, 0:3 * D], csil_b[:, b, :], wmod_s[:, 3 * D:6 * D],
                                   start=True, stop=True)
                ins.then_inc(s_modb, 1)

            def xn_transpose(g):
                pe.wait_ge(s_xn, g + 1)
                wait_turn_bank(pe, "ln1n", g)
                transpose_group(turn_bank("ln1n", g), lambda j: xn[:, g % 2, j, :]).then_inc(s_xnT, 1)

            def gate_products(g):
                if g == 0:
                    pe.wait_ge(s_wbd, 1)
                pe.wait_ge(s_hT, g + 1)
                if g >= 1:
                    pe.wait_ge(s_ta, g)
                t.matmul(bank[2][:, :], wx_bd[:, :], hT[:, cols(g)], start=True, stop=True)
                t.matmul(bank[3][:, :], wa_bd[:, :], hT[:, cols(g)], start=True, stop=True).then_inc(s_z, 1)

            def y_transpose(g):
                pe.wait_ge(s_y, g + 1)
                wait_turn_bank(pe, "scan", g)
                transpose_group(turn_bank("scan", g),
                                lambda j: yv[:, g * G + j * P:g * G + (j + 1) * P]).then_inc(s_yT, 1)

            def h2_transpose(g):
                pe.wait_ge(s_h2, g + 1)
                wait_turn_bank(pe, "ln2n", g)
                transpose_group(turn_bank("ln2n", g), lambda j: rows[:, g * GT + j, 0, 0:D]).then_inc(s_h2t, 1)

            def router(g):
                if g == 0:
                    pe.wait_ge(s_rw, 48)
                    pe.wait_ge(s_modrow, 1)
                pe.wait_ge(s_h2T, g + 1)
                for h in range(HC):
                    n = HC * g + h
                    if n >= 2:
                        pe.wait_ge(s_hr, n - 1)
                    t.matmul(bank[4 + h % 2][:, :], rw1_s[:, h * P:(h + 1) * P], h2T[:, g % 2, :],
                             start=True, stop=True).then_inc(s_rl1, 1)

            def logits(g):
                pe.wait_ge(s_hr, HC * (g + 1))
                if g == 0:
                    pe.wait_ge(s_const, 6)
                if g >= RG and g % RG == 0:
                    pe.wait_ge(s_lgc, g // RG)
                for j in range(GT):
                    n = (g % RG) * GT + j
                    o = bank[6][:, n * NE:(n + 1) * NE]
                    for h in range(HC):
                        t.matmul(o, hr[g % 2][:, h, j * P:(j + 1) * P], rw2_s[:, h, :], start=(h == 0), stop=False)
                    ins = t.matmul(o, ones_row[:, :], rb2_s[:, :], start=False, stop=True)
                ins.then_inc(s_lg, 1)

            def positions(r):
                pe.wait_ge(s_mask, r + 1)
                if r >= 1:
                    pe.wait_ge(s_slot, r)
                for j in range(RB):
                    o = bank[7][:, j * NE:(j + 1) * NE]
                    t.matmul(o, ones_bf[:, :], mcum_b[:, r, :], start=True, stop=False)
                    for i in range(j):
                        t.matmul(o, ones_bf[:, :], mboth[:, r * RB + i, :], start=False, stop=False)
                    ins = t.matmul(o, before[:, :], mboth[:, r * RB + j, :], start=False, stop=True)
                ins.then_inc(s_pos, 1)

            run({"setup": modulation, "ln1n": xn_transpose, "mod": gate_products, "scan": y_transpose,
                 "ln2n": h2_transpose, "rout": router, "logi": logits, "pos": positions})
            pe.wait_ge(s_slot, NR)
            t.matmul(bank[7][:, 0:NE], ones_bf[:, :], mcum_b[:, NR, :], start=True, stop=True).then_inc(s_cnt, 1)

            pe.wait_ge(s_w2, 16 * NE)
            pe.wait_ge(s_b2s, 16 * 3)
            pe.wait_ge(s_tab, 1)

            def turn_x(s, u):
                pe.wait_ge(s_xr[u], 16 * rounds(s, u))
                if not (static(s) and s < 2):
                    pe.wait_ge(s_xT, s - 1)
                for n in range(HALVES):
                    ins = t.transpose(bank[u % 2][:, n * P:(n + 1) * P], xr[:, u, n, 0:D], ident[:, :])
                ins.then_inc(s_txp, 1)

            def layer1(s, u):
                pe.wait_ge(s_w1t, s + 1)
                for h in range(HC):
                    if h % 2 == 0 and not (static(s) and s < 2):
                        pe.wait_ge(s_hs, 2 * (s - 2) + h // 2 + 1)
                    ins = t.matmul(bank[2 + 2 * (u % 2) + h // 2][:, (h % 2) * SL:(h % 2 + 1) * SL],
                                   w1_t[:, u % 2, h * P:(h + 1) * P], xT[:, u % 2, :], start=True, stop=True)
                    if h % 2:
                        ins.then_inc(s_l1, 1)

            def layer2(s, u, e):
                pe.wait_ge(s_hs, 2 * (s + 1))
                for n in range(HALVES):
                    if not (static(s) and s < 1):
                        pe.wait_ge(s_yo, HALVES * (s - 1) + n + 1)
                    o = bank[6 + n][:, 0:D]
                    for h in range(HC):
                        t.matmul(o, hsT[:, u % 2, h, n * P:(n + 1) * P], w2_s[:, bass.ds(e * (HC * D) + h * D, D)],
                                 start=(h == 0), stop=False)
                    t.matmul(o, ones_bf[0:3, :], b2_s[:, bass.ds(e * D, D)], start=False, stop=True).then_inc(s_l2, 1)

            def expert_of(s):
                return pe.value_load(tab_e[0:1, bass.ds(s, 1)], min_val=0, max_val=NE - 1)

            turn_x(0, 0)

            def step(s, u):
                if not static(s) or s + 1 < TILES:
                    turn_x(s + 1, (u + 1) % U)
                if not static(s) or s < TILES:
                    layer1(s, u)
                if not static(s) or s >= 1:
                    layer2(s - 1, (u - 1) % U, expert_of(s - 1))

            expert_steps(pe, step, TILES + 1)


_INS = ['L0_attn_x', 'L0_attn_a_param', 'L0_attn_w_in', 'L0_attn_w_a', 'L0_ffn_rw1', 'L0_ffn_rb1', 'L0_ffn_rw2',
        'L0_ffn_rb2', 'L0_ffn_w1', 'L0_ffn_b1', 'L0_ffn_w2', 'L0_ffn_b2', 'L0_c', 'L0_wmod']
_OUTS = [((2, 2048, 128), 'float32')]


def kernel(**inputs):
    import numpy as _np
    import concourse.bacc as _bacc
    from concourse import mybir as _mybir
    from concourse.bass_utils import run_bass_kernel_spmd as _run

    nc = _bacc.Bacc("TRN2", target_bir_lowering=False, num_devices=1)
    arrays, args = {}, []
    for name in _INS:
        a = _np.ascontiguousarray(inputs[name])
        arrays[f"in_{name}_dram"] = a
        args.append(nc.dram_tensor(f"in_{name}_dram", a.shape, _mybir.dt.from_np(a.dtype), kind="ExternalInput").ap())
    for i, (shape, dtype) in enumerate(_OUTS):
        dt = _mybir.dt.from_np(_np.dtype(dtype))
        args.append(nc.dram_tensor(f"out_{i}_dram", shape, dt, kind="ExternalOutput").ap())
    adaln_block(nc, *args)
    r = _run(nc, [arrays], core_ids=[0])
    got = tuple(r.results[0][f"out_{i}_dram"] for i in range(len(_OUTS)))
    return got[0]
```

```python
from contextlib import ExitStack

import concourse.bass as bass
from concourse import mybir

ALU = mybir.AluOpType
ACT = mybir.ActivationFunctionType
AX = mybir.AxisListType
F32 = mybir.dt.float32
BF16 = mybir.dt.bfloat16
I32 = mybir.dt.int32
U32 = mybir.dt.uint32

P = 128
EPS = 1e-5
GATE_FLOOR = 0.25


def adaln_block(nc, x, a_param, w_in, w_a, rw1, rb1, rw2, rb2, w1, b1, w2, b2, c, wmod, out):
    B, T, D = x.shape
    NH, HB, _ = w_in.shape
    HID = rw1.shape[1]
    NE = rw2.shape[1]
    TOK = B * T
    NT = TOK // P
    GT = 4
    G = GT * P
    NG = TOK // G
    GPB = NG // B
    HC = HID // P
    TOPK = 2
    HALVES = 2
    SL = HALVES * P
    REG = TOK + SL
    ROW = D + 2
    WE = HID + HC
    U = 4
    TILES = (TOPK * TOK + NE * (SL - 1)) // SL
    KT = TOK // SL
    assert D == P and HC == GT and B == 2 and NG == 8 and TILES >= 3 * U

    x_t = x.rearrange("b (n p) d -> p (b n) d", p=P)
    out_t = out.rearrange("b (n p) d -> p (b n) d", p=P)

    with ExitStack() as ctx:
        def sb(name, shape, dt=F32):
            return ctx.enter_context(nc.sbuf_tensor(name, shape, dt))

        def ps(name, shape, dt=F32):
            return ctx.enter_context(nc.psum_tensor(name, shape, dt))

        def sem(name):
            return ctx.enter_context(nc.semaphore(name))

        sorted_rows = nc.dram_tensor("sorted_rows", [NE * REG + SL, ROW], F32)
        expert_out = nc.dram_tensor("expert_out", [TOPK * TOK, D], F32)

        xs = sb("xs", [P, NT, D])
        wx_bd = sb("wx_bd", [P, P])
        wa_bd = sb("wa_bd", [P, P])
        rw1_s = sb("rw1_s", [P, HID])
        rw2_s = sb("rw2_s", [P, HC, NE])
        w1_s = sb("w1_s", [P, NE * WE])
        w2_s = sb("w2_s", [P, NE * HC * D])
        wmod_s = sb("wmod_s", [P, 6 * D])
        NSM = B + 1 + HC + NE * HC
        small = sb("small", [NSM, P])
        smallT = sb("smallT", [P, NSM])
        cT = smallT[:, 0:B]
        apar = smallT[:, B:B + 1]
        rb1_s = smallT[:, B + 1:B + 1 + HC]
        b1_c = smallT[:, B + 1 + HC:NSM].rearrange("p (e h) -> p e h", h=HC)
        wx_c = sb("wx_c", [P, HB])
        wa_c = sb("wa_c", [P, HB])
        csil = sb("csil", [P, 3, B])
        csil_b = sb("csil_b", [P, B, P])
        softp = sb("softp", [P, 8])
        modc = sb("modc", [P, 6, B])
        gac = sb("gac", [P, 3, B])
        sbB = sb("sbB", [P, B, D])
        cbB = sb("cbB", [P, B, D])
        gbB = sb("gbB", [P, B, D])
        gbS = sb("gbS", [P, B, D])
        ident = sb("ident", [P, P])
        before = sb("before", [P, P], BF16)
        ones_bf = sb("ones_bf", [P, P], BF16)
        ones_row = sb("ones_row", [1, P])
        half_neg = sb("half_neg", [P, GT])
        b2_in = sb("b2_in", [P, NE * D // P])
        b2_r = sb("b2_r", [P, 2, NE * D // P])
        b2_p = sb("b2_p", [P, 3, NE * D // P], BF16)
        b2_s = sb("b2_s", [3, NE * D], BF16)
        st1 = sb("st1", [P, NT, 6])
        mv1 = sb("mv1", [P, NT, 2])
        ve1 = sb("ve1", [P, NT])
        rs1 = sb("rs1", [P, NT])
        st2 = sb("st2", [P, NT, 6])
        mv2 = sb("mv2", [P, NT, 2])
        ve2 = sb("ve2", [P, NT])
        rs2 = sb("rs2", [P, NT])
        xn = sb("xn", [P, 2, GT, D])
        hT = sb("hT", [P, TOK])
        tx = sb("tx", [P, TOK])
        ta = sb("ta", [P, 2, G])
        av = sb("av", [P, TOK])
        qv = sb("qv", [P, TOK])
        yv = hT
        rows = sb("rows", [P, NT, TOPK, ROW])
        h2T = sb("h2T", [P, 2, G])
        hr = [z[:, 0:HC * G].rearrange("p (h t) -> p h t", h=HC) for z in (av, qv)]
        iota_i = sb("iota_i", [P, 256], I32)
        eid = sb("eid", [P, GT, NE])
        ereg = sb("ereg", [1, NE])
        lg = sb("lg", [P, GT, NE])
        best = sb("best", [P, GT, 8])
        bidx = sb("bidx", [P, GT, 8], U32)
        bidf = sb("bidf", [P, TOPK, GT])
        mk = sb("mk", [P, 2, TOPK, GT, NE])
        mboth = sb("mboth", [P, NG + 1, 1 + GT, NE], BF16)
        dlt = sb("dlt", [P, 2, GT])
        tdl = sb("tdl", [P, 2, GT])
        rb2_row = sb("rb2_row", [1, NE])
        rb2_b = sb("rb2_b", [P, NE])
        picked = sb("picked", [P, TOPK, GT, NE])
        slotf = sb("slotf", [P, TOPK, NT])
        sloti = sb("sloti", [P, TOPK, NT], I32)
        padr = sb("padr", [P, HALVES, ROW])
        cf = sb("cf", [1, NE])
        kslots = sb("kslots", [1, KT])
        tauf = sb("tauf", [1, TILES])
        cmpk = sb("cmpk", [1, NE, KT])
        te = sb("te", [1, NE])
        sinc = sb("sinc", [1, NE])
        one8 = sb("one8", [1, NE])
        cmpt = sb("cmpt", [1, TILES, NE])
        cmpu = sb("cmpu", [1, TILES, NE])
        tf = sb("tf", [1, 5, TILES])
        tab_row = sb("tab_row", [1, TILES], I32)
        tab_e = sb("tab_e", [1, TILES], I32)
        pad_f = sb("pad_f", [1, NE])
        pad_i = sb("pad_i", [1, NE], I32)
        spare = [0]

        def in_tx(n):
            spare[0] += n
            assert spare[0] <= TOK
            return tx[:, spare[0] - n:spare[0]]

        xr = in_tx(U * HALVES * ROW).rearrange("p (u n r) -> p u n r", u=U, n=HALVES)
        hsT = in_tx(2 * HC * SL).rearrange("p (r h t) -> p r h t", r=2, h=HC)
        yo = in_tx(2 * HALVES * D).rearrange("p (r n d) -> p r n d", r=2, n=HALVES)
        xT = h2T[:, :, 0:SL]
        prob_t = sb("prob_t", [P, U, HALVES, 1])
        dest_t = sb("dest_t", [P, U, HALVES, 1], I32)
        w1_t = sb("w1_t", [P, 2, WE])
        y01 = [z[:, i * TOPK * G:(i + 1) * TOPK * G].rearrange("p (k n d) -> p k n d", k=TOPK, d=D)
               for z in (av, qv) for i in range(NG // 2)]

        bank = [ps(f"bank{i}", [P, 512]) for i in range(8)]

        def sems(*names):
            return [sem(n) for n in names]

        s_x = sems(*(f"s_x{g}" for g in range(NG)))
        s_small, s_wmod, s_wc, s_rw, s_w1, s_w2, s_b2in, s_b2s = sems(
            "s_small", "s_wmod", "s_wc", "s_rw", "s_w1", "s_w2", "s_b2in", "s_b2s")
        s_zero, s_ident, s_const, s_wsel, s_wbd, s_turned, s_cols, s_absa, s_ecs, s_esp, s_cs = sems(
            "s_zero", "s_ident", "s_const", "s_wsel", "s_wbd", "s_turned", "s_cols", "s_absa", "s_ecs",
            "s_esp", "s_cs")
        s_modc, s_modb, s_modok, s_softp, s_modrow, s_b2p, s_dve = sems(
            "s_modc", "s_modb", "s_modok", "s_softp", "s_modrow", "s_b2p", "s_dve")
        s_var1, s_rstd1, s_xn, s_xnT, s_hT, s_z, s_ta, s_exp, s_u, s_m, s_y, s_yT = sems(
            "s_var1", "s_rstd1", "s_xn", "s_xnT", "s_hT", "s_z", "s_ta", "s_exp", "s_u", "s_m", "s_y", "s_yT")
        s_in = sem("s_in")
        s_res, s_var2, s_rstd2, s_h2, s_h2t, s_h2T, s_dup, s_rl1, s_hr, s_lg, s_lgc, s_mask, s_pos = sems(
            "s_res", "s_var2", "s_rstd2", "s_h2", "s_h2t", "s_h2T", "s_dup", "s_rl1", "s_hr", "s_lg", "s_lgc",
            "s_mask", "s_pos")
        s_dlt, s_tdl, s_slot, s_disp, s_cnt, s_tab, s_pad = sems(
            "s_dlt", "s_tdl", "s_slot", "s_disp", "s_cnt", "s_tab", "s_pad")
        s_xr = sems(*(f"s_xr{i}" for i in range(U)))
        s_txp, s_xT, s_w1t, s_l1, s_hs, s_l2, s_yo, s_fin = sems(
            "s_txp", "s_xT", "s_w1t", "s_l1", "s_hs", "s_l2", "s_yo", "s_fin")
        s_taken, s_out = sems("s_taken", "s_out")
        s_sc = sems(*(f"s_sc{i}" for i in range(U)))
        s_y01 = sems(*(f"s_y01_{g}" for g in range(NG)))

        rows_i = rows[:, :, :, :].bitcast(I32)
        padr_i = padr[:, :, :].bitcast(I32)
        xr_i = xr.bitcast(I32)
        block = ctx.enter_context(nc.Block())

        def cols(g):
            return slice(g * G, (g + 1) * G)

        def tiles(g):
            return slice(g * GT, (g + 1) * GT)

        PLAN = {
            "tensor": """
                setup:0 modrow:0 turn_x:0 turn_x:1 gates:0 turn_x:2 turn_x:3 gates:1 gates:2 gates:3 turn_x:4 turn_x:5
                gates:4 gates:5 turn_x:6 turn_x:7 turn_y:0 gates:6 turn_y:1 gates:7 turn_y:2 turn_h:0 router:0 turn_y:3
                turn_h:1 turn_h:2 logits:0 router:1 rank:0 turn_y:4 logits:1 router:2 rank:1 turn_h:3 logits:2 turn_y:5
                router:3 rank:2 turn_h:4 logits:3 turn_y:6 router:4 rank:3 turn_h:5 logits:4 turn_y:7 router:5 rank:4
                turn_h:6 logits:5 router:6 rank:5 turn_h:7 logits:6 router:7 rank:6 logits:7 rank:7""",
            "vector": """
                stats1:0 stats1:1 stats1:2 stats1:3 stats1:4 stats1:5 setup:0 norm1:0 norm1:1 norm1:2 norm1:3 late:0
                norm1:4 norm1:5 input:0 input:1 input:2 input:3 stats1:6 stats1:7 norm1:6 norm1:7 scan:0 scan:1 stats2:0
                scan:2 norm2:0 scan:3 stats2:1 stats2:2 norm2:1 norm2:2 stats2:3 input:4 scan:4 top2:0 norm2:3 place:0
                stats2:4 top2:1 input:5 scan:5 place:1 norm2:4 top2:2 stats2:5 input:6 place:2 scan:6 norm2:5 top2:3
                stats2:6 place:3 input:7 scan:7 top2:4 norm2:6 stats2:7 place:4 norm2:7 top2:5 place:5 top2:6 place:6
                top2:7 place:7""",
            "scalar": """
                modulate:0 modulate:1 tanh:0 modulate:2 modulate:3 decay:0 tanh:1 decay:1 tanh:2 tanh:3 decay:2 decay:3
                modulate:4 modulate:5 mult:0 tanh:4 modulate:6 tanh:5 modulate:7 decay:4 tanh:6 decay:5 tanh:7 decay:6
                decay:7 dup:0 copy:0 mult:1 silu:0 copy:1 copy:2 dup:1 dup:2 silu:1 share:0 dup:3 silu:2 share:1 copy:3
                dup:4 silu:3 share:2 copy:4 silu:4 share:3 copy:5 dup:5 silu:5 share:4 dup:6 copy:6 silu:6 share:5
                copy:7 dup:7 silu:7 share:6 share:7""",
            "gpsimd": """
                rstd1:0 rstd1:1 rstd1:2 rstd1:3 const:0 rstd1:4 rstd1:5 clamp:0 clamp:1 clamp:2 clamp:3 rstd1:6 rstd1:7
                rstd2:0 clamp:4 clamp:5 clamp:6 clamp:7 rstd2:1 rstd2:2 rstd2:3 send:0 rstd2:4 send:1 send:2 send:3
                rstd2:5 send:4 send:5 rstd2:6 send:6 send:7 rstd2:7 send:8 send:9 send:10 send:11 send:12 send:13
                send:14 send:15""",
        }
        PLAN = {engine: [(part.split(":")[0], int(part.split(":")[1])) for part in parts.split()]
                for engine, parts in PLAN.items()}

        def run(engine, parts):
            for name, n in PLAN[engine]:
                parts[name](n)

        READ = {"turn_x": s_hT, "turn_y": s_res, "turn_h": s_h2T}
        TURNS = [part for part in PLAN["tensor"] if part[0] in READ]

        def turn_bank(name, g):
            return bank[TURNS.index((name, g)) % 2]

        def wait_turn_bank(pe, name, g):
            n = TURNS.index((name, g))
            if n >= 2:
                before_name, before_g = TURNS[n - 2]
                pe.wait_ge(READ[before_name], before_g + 1)

        LOOPS = (TILES - 3) // U

        def expert_steps(eng, body, last):
            for s in range(U):
                body(s, s)
            with eng.Fori(1, LOOPS) as n:
                for u in range(U):
                    body(n * U + u, u)
            for s in range(LOOPS * U, last):
                body(s, s % U)

        def static(s):
            return isinstance(s, int)

        def rounds(s, u):
            return (s - u) // U + 1

        @block.sync
        def _(sp):
            sp.dma_start(xs[:, tiles(0), :], x_t[:, tiles(0), :]).then_inc(s_x[0], 16)
            sp.dma_start(wmod_s[:, :], wmod).then_inc(s_wmod, 16)
            for g in range(1, GPB):
                sp.dma_start(xs[:, tiles(g), :], x_t[:, tiles(g), :]).then_inc(s_x[g], 16)
            sp.dma_start(rw1_s[:, :], rw1).then_inc(s_rw, 16)
            sp.dma_start(rw2_s[:, :, :], rw2.rearrange("(c p) e -> p c e", p=P)).then_inc(s_rw, 16)
            sp.dma_start(rb2_row[:, :], rb2.rearrange("(a e) -> a e", a=1)).then_inc(s_rw, 16)
            sp.dma_start(b2_in[:, :], b2.rearrange("e (q n) -> (e q) n", q=P // NE)).then_inc(s_b2in, 16)
            for g in range(GPB, NG):
                sp.dma_start(xs[:, tiles(g), :], x_t[:, tiles(g), :]).then_inc(s_x[g], 16)
            for e in range(NE):
                sp.dma_start(w1_s[:, e * WE:e * WE + HID], w1[e]).then_inc(s_w1, 16)
                sp.dma_start(w2_s[:, e * HC * D:(e + 1) * HC * D].rearrange("p (c d) -> p c d", c=HC),
                             w2[e].rearrange("(c p) d -> p c d", p=P)).then_inc(s_w2, 16)
            sp.wait_ge(s_b2p, 1)
            for k in range(3):
                sp.dma_start(b2_s[k:k + 1, :], b2_p[:, k, :]).then_inc(s_b2s, 16)

            def padding(row):
                sp.dma_start(sorted_rows[row, :].rearrange("(n p) r -> p n r", p=P),
                             padr[:, :, :]).then_inc(s_pad, 16)

            sp.wait_ge(s_const, 7)
            padding(slice(NE * REG, NE * REG + SL))
            sp.wait_ge(s_tab, 1)
            for e in range(NE):
                padding(bass.ds(sp.value_load(pad_i[0:1, e:e + 1], min_val=e * REG, max_val=e * REG + TOK), SL))
            sp.wait_ge(s_pad, 16 * (NE + 1))
            sp.wait_ge(s_disp, 16 * TOPK * NT)

            def load(s, u):
                r = sp.value_load(tab_row[0:1, bass.ds(s, 1)], min_val=0, max_val=NE * REG)
                if not (static(s) and s < U):
                    sp.wait_ge(s_taken, s - U + 1)
                sp.dma_start(xr[:, u, :, :], sorted_rows[bass.ds(r, SL), :]
                             .rearrange("(n p) r -> p n r", p=P)).then_inc(s_xr[u], 16)

            expert_steps(sp, load, TILES)
            for u in range(U):
                sp.wait_ge(s_sc[u], 16 * HALVES * ((TILES - 1 - u) // U + 1))
            for g in range(NG):
                for k in range(TOPK):
                    sp.dma_start(y01[g][:, k, :, :],
                                 expert_out[k * TOK + g * G:k * TOK + (g + 1) * G, :]
                                 .rearrange("(n p) d -> p n d", p=P)).then_inc(s_y01[g], 16)

        @block.gpsimd
        def _(pool):
            p = nc.gpsimd
            p.memset(ident[:, :], 0.0).then_inc(s_zero, 1)
            p.memset(half_neg[:, :], -0.5).then_inc(s_const, 1)
            pool.wait_ge(s_zero, 1)
            p.affine_select(out=ident[:, :], in_=ident[:, :], compare_op=ALU.not_equal, fill=1.0,
                            base=0, pattern=[[-1, P]], channel_multiplier=1).then_inc(s_ident, 1)
            pool.wait_ge(s_wc, 32)
            for w_c, w_bd in ((wx_c, wx_bd), (wa_c, wa_bd)):
                blocks = w_bd[:, :].rearrange("p (h e) -> p h e", h=NH)
                ins = p.affine_select(out=blocks, in_=w_c[:, :].unsqueeze(1).to_broadcast([P, NH, HB]),
                                      compare_op=ALU.is_ge, fill=0.0, base=0, pattern=[[-HB, NH], [0, HB]],
                                      channel_multiplier=1)
            ins.then_inc(s_wsel, 1)
            pool.wait_ge(s_wsel, 1)
            for w_bd in (wx_bd, wa_bd):
                blocks = w_bd[:, :].rearrange("p (h e) -> p h e", h=NH)
                ins = p.affine_select(out=blocks, in_=blocks, compare_op=ALU.is_ge, fill=0.0, base=HB - 1,
                                      pattern=[[HB, NH], [0, HB]], channel_multiplier=-1)
            ins.then_inc(s_wbd, 1)

            def rstd1(g):
                pool.wait_ge(s_var1, g + 1)
                p.tensor_tensor(rs1[:, tiles(g)], ve1[:, tiles(g)], half_neg[:, :], ALU.pow).then_inc(s_rstd1, 1)

            def clamp(g):
                pool.wait_ge(s_exp, g + 1)
                p.tensor_scalar(qv[:, cols(g)], qv[:, cols(g)], 1.0, None, ALU.min).then_inc(s_u, 1)

            def constants(_):
                p.memset(before[:, :], 1.0).then_inc(s_zero, 1)
                pool.wait_ge(s_zero, 2)
                p.affine_select(out=before[:, :], in_=before[:, :], compare_op=ALU.is_gt, fill=0.0,
                                base=0, pattern=[[1, P]], channel_multiplier=-1).then_inc(s_const, 1)
                p.memset(ones_bf[:, :], 1.0).then_inc(s_const, 1)
                p.memset(ones_row[:, :], 1.0).then_inc(s_const, 1)
                p.iota(iota_i[:, 0:GT * NE], pattern=[[0, GT], [1, NE]], base=0, channel_multiplier=0)
                p.iota(iota_i[0:1, 64:64 + KT], pattern=[[SL, KT]], base=0, channel_multiplier=0)
                p.iota(iota_i[0:1, 128:128 + TILES], pattern=[[1, TILES]], base=0,
                       channel_multiplier=0).then_inc(s_const, 1)
                for k in range(TOPK):
                    ins = p.iota(rows_i[:, :, k, D + 1], pattern=[[P, NT]], base=k * TOK, channel_multiplier=1)
                ins.then_inc(s_const, 1)
                p.memset(padr[:, :, :], 0.0).then_inc(s_zero, 1)
                pool.wait_ge(s_zero, 3)
                p.iota(padr_i[:, :, D + 1], pattern=[[P, HALVES]], base=TOPK * TOK,
                       channel_multiplier=1).then_inc(s_const, 1)

            def rstd2(g):
                pool.wait_ge(s_var2, g + 1)
                p.tensor_tensor(rs2[:, tiles(g)], ve2[:, tiles(g)], half_neg[:, :], ALU.pow).then_inc(s_rstd2, 1)

            def dispatch(n):
                pool.wait_ge(s_slot, 2 * n // GT + 1)
                pool.wait_ge(s_dup, 2 * n // GT + 1)
                for t in (2 * n, 2 * n + 1):
                    for k in range(TOPK):
                        p.indirect_dma_start(
                            sorted_rows[:, :], bass.IndirectOffsetOnAxis(ap=sloti[:, k, t:t + 1], axis=0),
                            rows[:, t, k, :], None).then_inc(s_disp, 16)

            run("gpsimd", {"rstd1": rstd1, "const": constants, "clamp": clamp, "rstd2": rstd2, "send": dispatch})

            last_row = pool.to_reg(TOPK * TOK - 1)
            for s in range(TILES):
                for n in range(HALVES):
                    pool.wait_ge(s_yo, HALVES * s + n + 1)
                    p.indirect_dma_start(
                        expert_out[:, :], bass.IndirectOffsetOnAxis(ap=dest_t[:, s % U, n, :], axis=0),
                        yo[:, s % 2, n, :], None, bounds_check=last_row, oob_is_err=False).then_inc(s_sc[s % U], 16)

        @block.scalar
        def _(act):
            act.dma_start(small[0:B, :], c).then_inc(s_small, 16)
            act.dma_start(small[B:B + 1, :], a_param.rearrange("(a p) -> a p", a=1)).then_inc(s_small, 16)
            act.dma_start(small[B + 1:B + 1 + HC, :], rb1.rearrange("(h p) -> h p", p=P)).then_inc(s_small, 16)
            act.dma_start(small[B + 1 + HC:NSM, :], b1.rearrange("e (h p) -> (e h) p", p=P)).then_inc(s_small, 16)
            act.dma_start(wx_c[:, :], w_in.rearrange("h d e -> (h d) e")).then_inc(s_wc, 16)
            act.dma_start(wa_c[:, :], w_a.rearrange("h d e -> (h d) e")).then_inc(s_wc, 16)
            act.wait_ge(s_cols, 1)
            nc.scalar.activation(csil[:, 0, :], cT, ACT.Exp, scale=-1.0).then_inc(s_ecs, 1)
            act.wait_ge(s_absa, 1)
            nc.scalar.activation(softp[:, 1:2], softp[:, 0:1], ACT.Exp, scale=-1.0).then_inc(s_esp, 1)

            def modulate(g):
                act.wait_ge(s_xnT, g + 1)
                if g == 0:
                    act.wait_ge(s_modok, 1)
                b = g // GPB
                nc.scalar.activation(hT[:, cols(g)], turn_bank("turn_x", g)[:, :], ACT.Identity,
                                     bias=modc[:, 0, b:b + 1], scale=gac[:, 0, b:b + 1]).then_inc(s_hT, 1)

            def gates(g):
                act.wait_ge(s_z, g + 1)
                if g >= 2:
                    act.wait_ge(s_exp, g - 1)
                z = 2 + 2 * (g % 2)
                nc.scalar.activation(tx[:, cols(g)], bank[z][:, :], ACT.Tanh, scale=0.5)
                nc.scalar.activation(ta[:, g % 2, :], bank[z + 1][:, :], ACT.Tanh, scale=0.5).then_inc(s_ta, 1)

            def decay(g):
                if g == 0:
                    act.wait_ge(s_softp, 1)
                act.wait_ge(s_ta, g + 1)
                nc.scalar.activation(av[:, cols(g)], ta[:, g % 2, :], ACT.Exp, bias=softp[:, 6:7],
                                     scale=softp[:, 6:7])
                nc.scalar.activation(qv[:, cols(g)], ta[:, g % 2, :], ACT.Exp, bias=softp[:, 7:8],
                                     scale=softp[:, 7:8]).then_inc(s_exp, 1)

            def multiplier(b):
                for g in range(b * GPB, (b + 1) * GPB):
                    act.wait_ge(s_u, g + 1)
                    nc.scalar.activation(qv[:, cols(g)], qv[:, cols(g)], ACT.Sqrt, bias=gac[:, 2, 0:1],
                                         scale=-0.25).then_inc(s_m, 1)

            def router_copy(g):
                act.wait_ge(s_h2t, g + 1)
                if g >= 2:
                    act.wait_ge(s_rl1, HC * (g - 1))
                nc.scalar.copy(h2T[:, g % 2, :], turn_bank("turn_h", g)[:, :]).then_inc(s_h2T, 1)

            def duplicate(g):
                act.wait_ge(s_h2, g + 1)
                nc.scalar.copy(rows[:, tiles(g), 1, 0:D], rows[:, tiles(g), 0, 0:D]).then_inc(s_dup, 1)

            def router_silu(g):
                if g >= 2:
                    act.wait_ge(s_lg, g - 1)
                for h in range(HC):
                    act.wait_ge(s_rl1, HC * g + h + 1)
                    nc.scalar.activation(hr[g % 2][:, h, :], bank[2 + h][:, :], ACT.Silu,
                                         bias=rb1_s[:, h:h + 1]).then_inc(s_hr, 1)

            def second_share(g):
                act.wait_ge(s_dlt, g + 1)
                nc.scalar.activation(tdl[:, g % 2, :], dlt[:, g % 2, :], ACT.Tanh, scale=0.5).then_inc(s_tdl, 1)

            run("scalar", {"modulate": modulate, "tanh": gates, "decay": decay, "mult": multiplier,
                           "copy": router_copy, "dup": duplicate, "silu": router_silu, "share": second_share})

            def hidden(s, u):
                for q in range(2):
                    act.wait_ge(s_l1, 2 * s + q + 1)
                    if q == 0 and not (static(s) and s < 2):
                        act.wait_ge(s_l2, HALVES * (s - 1))
                    for h in (2 * q, 2 * q + 1):
                        ins = nc.scalar.activation(
                            hsT[:, u % 2, h, :], bank[2 + 2 * (u % 2) + q][:, (h % 2) * SL:(h % 2 + 1) * SL],
                            ACT.Silu, bias=w1_t[:, u % 2, HID + h:HID + h + 1])
                    ins.then_inc(s_hs, 1)

            expert_steps(act, hidden, TILES)

            for g in range(NG):
                act.wait_ge(s_fin, g + 1)
                act.dma_start(out_t[:, tiles(g), :], y01[g][:, 0, :, :]).then_inc(s_out, 16)
            act.wait_ge(s_out, 16 * NG)

        @block.vector
        def _(dve):
            chain = [0]

            def link(ins):
                chain[0] += 1
                ins.then_inc(s_dve, 1)
                dve.wait_ge(s_dve, chain[0])

            v = nc.vector

            def stats(st, mv, ve, g, done):
                for t in range(g * GT, (g + 1) * GT):
                    ins = v.bn_stats(st[:, t, :], xs[:, t, :])
                link(ins)
                for t in range(g * GT, (g + 1) * GT):
                    ins = v.bn_aggr(mv[:, t, :], st[:, t, :])
                link(ins)
                v.tensor_scalar(ve[:, tiles(g)], mv[:, tiles(g), 1], EPS, None, ALU.add).then_inc(done, 1)

            def ln1_stats(g):
                dve.wait_ge(s_x[g], 16)
                stats(st1, mv1, ve1, g, s_var1)

            def ln1_norm(g):
                dve.wait_ge(s_rstd1, g + 1)
                if g >= 2:
                    dve.wait_ge(s_xnT, g - 1)
                for j in range(GT):
                    t = g * GT + j
                    ins = v.tensor_scalar(xn[:, g % 2, j, :], xs[:, t, :], mv1[:, t, 0:1], rs1[:, t:t + 1],
                                          ALU.subtract, ALU.mult)
                ins.then_inc(s_xn, 1)

            def setup(_):
                dve.wait_ge(s_turned, 1)
                v.tensor_copy(smallT[:, :], bank[7][:, 0:NSM]).then_inc(s_cols, 1)
                dve.wait_ge(s_cols, 1)
                v.scalar_tensor_tensor(softp[:, 0:1], apar, -1.0, apar, ALU.mult, ALU.max).then_inc(s_absa, 1)
                dve.wait_ge(s_ecs, 1)
                link(v.tensor_scalar(csil[:, 1, :], csil[:, 0, :], 1.0, None, ALU.add))
                link(v.reciprocal(csil[:, 2, :], csil[:, 1, :]))
                link(v.tensor_tensor(csil[:, 0, :], cT, csil[:, 2, :], ALU.mult))
                v.tensor_copy(csil_b[:, :, :], csil[:, 0, :].unsqueeze(2).to_broadcast([P, B, P])).then_inc(s_cs, 1)
                softplus()
                dve.wait_ge(s_modc, 1)
                link(v.tensor_copy(modc[:, :, :], bank[6][:, 0:6 * B].rearrange("p (i b) -> p i b", b=B)))
                v.memset(gac[:, 2, :], 0.25)
                v.tensor_scalar(gac[:, 0, :], modc[:, 1, :], 1.0, None, ALU.add).then_inc(s_modok, 1)

            def softplus():
                dve.wait_ge(s_esp, 1)
                link(v.tensor_scalar(softp[:, 2:3], softp[:, 1:2], 2.0, None, ALU.add))
                link(v.reciprocal(softp[:, 3:4], softp[:, 2:3]))
                link(v.tensor_tensor(softp[:, 2:3], softp[:, 1:2], softp[:, 3:4], ALU.mult))
                link(v.tensor_tensor(softp[:, 3:4], softp[:, 2:3], softp[:, 2:3], ALU.mult))
                link(v.tensor_scalar(softp[:, 4:5], softp[:, 3:4], 1 / 17, 1 / 15, ALU.mult, ALU.add))
                for k in range(13, 0, -2):
                    link(v.tensor_scalar(softp[:, 4:5], softp[:, 4:5], softp[:, 3:4], 1 / k, ALU.mult, ALU.add))
                link(v.tensor_scalar(softp[:, 5:6], apar, 0.0, 0.5, ALU.max, ALU.mult))
                link(v.tensor_scalar(softp[:, 4:5], softp[:, 4:5], softp[:, 2:3], softp[:, 5:6], ALU.mult, ALU.add))
                v.tensor_scalar(softp[:, 6:7], softp[:, 4:5], -8.0, None, ALU.mult)
                v.tensor_scalar(softp[:, 7:8], softp[:, 4:5], -16.0, None, ALU.mult).then_inc(s_softp, 1)

            def gated_inputs(g):
                dve.wait_ge(s_ta, g + 1)
                v.scalar_tensor_tensor(tx[:, cols(g)], tx[:, cols(g)], 1.0, hT[:, cols(g)],
                                       ALU.add, ALU.mult).then_inc(s_in, 1)

            def scan(g):
                b = g // GPB
                dve.wait_ge(s_in, g + 1)
                dve.wait_ge(s_m, g + 1)
                link(v.scalar_tensor_tensor(tx[:, cols(g)], tx[:, cols(g)], gac[:, 1, b:b + 1], qv[:, cols(g)],
                                            ALU.mult, ALU.mult))
                if g % GPB:
                    dve.wait_ge(s_y, g)
                init = 0.0 if g % GPB == 0 else yv[:, g * G - 1:g * G]
                v.tensor_tensor_scan(yv[:, cols(g)], av[:, cols(g)], tx[:, cols(g)], init,
                                     ALU.mult, ALU.add).then_inc(s_y, 1)

            def residual(g):
                dve.wait_ge(s_yT, g + 1)
                v.tensor_tensor(xs[:, tiles(g), :], turn_bank("turn_y", g)[:, :].rearrange("p (n d) -> p n d", d=D),
                                xs[:, tiles(g), :], ALU.add).then_inc(s_res, 1)
                dve.wait_ge(s_res, g + 1)

            def ln2_norm(g):
                b = g // GPB
                dve.wait_ge(s_rstd2, g + 1)
                for j in range(GT):
                    t = g * GT + j
                    ins = v.scalar_tensor_tensor(rows[:, t, 0, 0:D], xs[:, t, :], mv2[:, t, 0:1], cbB[:, b, :],
                                                 ALU.subtract, ALU.mult)
                link(ins)
                for j in range(GT):
                    t = g * GT + j
                    ins = v.scalar_tensor_tensor(rows[:, t, 0, 0:D], rows[:, t, 0, 0:D], rs2[:, t:t + 1],
                                                 sbB[:, b, :], ALU.mult, ALU.add)
                ins.then_inc(s_h2, 1)

            def top2(g):
                dve.wait_ge(s_lg, g + 1)
                v.tensor_tensor(lg[:, :, :], bank[6][:, 0:GT * NE].rearrange("p (j e) -> p j e", e=NE),
                                rb2_b[:, :].unsqueeze(1).to_broadcast([P, GT, NE]), ALU.add).then_inc(s_lgc, 1)
                dve.wait_ge(s_lgc, g + 1)
                for j in range(GT):
                    ins = v.max(best[:, j, :], lg[:, j, :])
                link(ins)
                for j in range(GT):
                    ins = v.max_index(bidx[:, j, :], best[:, j, :], lg[:, j, :])
                link(ins)
                v.tensor_tensor(dlt[:, g % 2, :], best[:, :, 1], best[:, :, 0], ALU.subtract).then_inc(s_dlt, 1)
                link(v.tensor_copy(bidf[:, :, :], bidx[:, :, 0:TOPK].rearrange("p j k -> p k j")))
                m = mk[:, g % 2, :, :, :]
                link(v.tensor_tensor(m, eid[:, :, :].unsqueeze(1).to_broadcast([P, TOPK, GT, NE]),
                                     bidf[:, :, :].unsqueeze(3).to_broadcast([P, TOPK, GT, NE]), ALU.is_equal))
                link(v.tensor_tensor(mboth[:, g, 1:, :], m[:, 0, :, :], m[:, 1, :, :], ALU.add))
                with nc.allow_low_precision(reason="whole numbers no larger than NT"):
                    v.tensor_reduce(mboth[:, g + 1, 0, :], mboth[:, g, :, :].rearrange("p j e -> p e j"),
                                    AX.X, ALU.add).then_inc(s_mask, 1)
                dve.wait_ge(s_mask, g + 1)

            def place(g):
                dve.wait_ge(s_tdl, g + 1)
                v.tensor_scalar(rows[:, tiles(g), 0, D], tdl[:, g % 2, :], -0.5, 0.5, ALU.mult, ALU.add)
                v.tensor_scalar(rows[:, tiles(g), 1, D], tdl[:, g % 2, :], 0.5, 0.5, ALU.mult, ALU.add)
                dve.wait_ge(s_pos, g + 1)
                place_of = bank[7][:, 0:GT * NE].rearrange("p (j e) -> p j e", e=NE)
                for k in range(TOPK):
                    ins = v.tensor_tensor(picked[:, k, :, :], place_of, mk[:, g % 2, k, :, :], ALU.mult)
                link(ins)
                link(v.tensor_reduce(slotf[:, :, tiles(g)], picked[:, :, :, :], AX.X, ALU.add))
                v.tensor_copy(sloti[:, :, tiles(g)], slotf[:, :, tiles(g)]).then_inc(s_slot, 1)

            def late(_):
                link(v.tensor_scalar(gac[:, 1, :], modc[:, 2, :], 0.0, 2.0, ALU.is_ge, ALU.mult))
                link(v.scalar_tensor_tensor(modc[:, 2, :], modc[:, 2, :], -1.0, modc[:, 2, :], ALU.mult, ALU.max))
                link(v.tensor_scalar(modc[:, 2, :], modc[:, 2, :], GATE_FLOOR, None, ALU.max))
                link(v.scalar_tensor_tensor(gac[:, 1, :], gac[:, 1, :], -1.0, modc[:, 2, :], ALU.add, ALU.mult))
                dve.wait_ge(s_modb, 1)
                v.tensor_copy(rb2_b[:, :], bank[6][:, 3 * D:3 * D + NE])
                for b in range(B):
                    m = bank[6 + b]
                    v.tensor_copy(sbB[:, b, :], m[:, 0:D])
                    v.tensor_scalar(cbB[:, b, :], m[:, D:2 * D], 1.0, None, ALU.add)
                    v.tensor_scalar(gbS[:, b, :], m[:, 2 * D:3 * D], 0.0, 2.0, ALU.is_ge, ALU.mult)
                    ins = v.tensor_copy(gbB[:, b, :], m[:, 2 * D:3 * D])
                ins.then_inc(s_modrow, 1)
                dve.wait_ge(s_modrow, 1)
                link(v.scalar_tensor_tensor(gbB[:, :, :], gbB[:, :, :], -1.0, gbB[:, :, :], ALU.mult, ALU.max))
                link(v.tensor_scalar(gbB[:, :, :], gbB[:, :, :], GATE_FLOOR, None, ALU.max))
                link(v.scalar_tensor_tensor(gbB[:, :, :], gbS[:, :, :], -1.0, gbB[:, :, :], ALU.add, ALU.mult))
                dve.wait_ge(s_b2in, 16)
                link(v.tensor_copy(b2_p[:, 0, :], b2_in[:, :]))
                link(v.tensor_tensor(b2_r[:, 0, :], b2_in[:, :], b2_p[:, 0, :], ALU.subtract))
                link(v.tensor_copy(b2_p[:, 1, :], b2_r[:, 0, :]))
                link(v.tensor_tensor(b2_r[:, 1, :], b2_r[:, 0, :], b2_p[:, 1, :], ALU.subtract))
                v.tensor_copy(b2_p[:, 2, :], b2_r[:, 1, :]).then_inc(s_b2p, 1)
                v.tensor_copy(w1_s[:, :].rearrange("p (e w) -> p e w", e=NE)[:, :, HID:WE], b1_c)
                constants()

            def constants():
                dve.wait_ge(s_const, 5)
                v.tensor_copy(eid[:, :, :], iota_i[:, 0:GT * NE].rearrange("p (j e) -> p j e", e=NE))
                v.tensor_copy(kslots[:, :], iota_i[0:1, 64:64 + KT])
                v.tensor_copy(tauf[:, :], iota_i[0:1, 128:128 + TILES])
                v.memset(mboth[:, 0, 0, :], 0.0)
                link(v.memset(one8[:, :], 1.0))
                link(v.tensor_scalar(ereg[:, :], eid[0:1, 0, :], float(REG), None, ALU.mult))

            def residual_stats(g):
                residual(g)
                stats(st2, mv2, ve2, g, s_var2)

            run("vector", {"stats1": ln1_stats, "setup": setup, "norm1": ln1_norm, "input": gated_inputs,
                           "late": late, "scan": scan, "stats2": residual_stats, "norm2": ln2_norm,
                           "top2": top2, "place": place})

            dve.wait_ge(s_cnt, 1)
            link(v.tensor_copy(cf[:, :], bank[7][0:1, 0:NE]))
            link(v.tensor_tensor(cmpk[:, :, :], cf[:, :].unsqueeze(2).to_broadcast([1, NE, KT]),
                                 kslots[:, :].unsqueeze(1).to_broadcast([1, NE, KT]), ALU.is_gt))
            link(v.tensor_reduce(te[:, :], cmpk[:, :, :], AX.X, ALU.add))
            link(v.tensor_tensor_scan(sinc[:, :], one8[:, :], te[:, :], 0.0, ALU.mult, ALU.add))
            link(v.tensor_tensor(cmpt[:, :, :], tauf[:, :].unsqueeze(2).to_broadcast([1, TILES, NE]),
                                 sinc[:, :].unsqueeze(1).to_broadcast([1, TILES, NE]), ALU.is_ge))
            link(v.tensor_tensor(cmpu[:, :, :], cmpt[:, :, :],
                                 te[:, :].unsqueeze(1).to_broadcast([1, TILES, NE]), ALU.mult))
            link(v.tensor_reduce(tf[:, 0, :], cmpt[:, :, :], AX.X, ALU.add))
            link(v.tensor_reduce(tf[:, 1, :], cmpu[:, :, :], AX.X, ALU.add))
            link(v.tensor_tensor(tf[:, 2, :], tauf[:, :], tf[:, 1, :], ALU.subtract))
            link(v.tensor_scalar(tf[:, 3, :], tf[:, 0, :], float(REG), None, ALU.mult))
            link(v.scalar_tensor_tensor(tf[:, 4, :], tf[:, 2, :], float(SL), tf[:, 3, :], ALU.mult, ALU.add))
            v.tensor_scalar(tab_row[:, :], tf[:, 4, :], float(NE * REG), None, ALU.min)
            v.tensor_scalar(tab_e[:, :], tf[:, 0, :], float(NE - 1), None, ALU.min)
            link(v.tensor_tensor(pad_f[:, :], cf[:, :], ereg[:, :], ALU.add))
            v.tensor_copy(pad_i[:, :], pad_f[:, :]).then_inc(s_tab, 1)

            def prepare(s, u, e):
                dve.wait_ge(s_txp, s + 1)
                if not (static(s) and s < 2):
                    dve.wait_ge(s_l1, 2 * (s - 1))
                    dve.wait_ge(s_hs, 2 * (s - 1))
                v.tensor_copy(xT[:, u % 2, :], bank[u % 2][:, 0:SL]).then_inc(s_xT, 1)
                if not (static(s) and s < U):
                    dve.wait_ge(s_sc[u], 16 * HALVES * (rounds(s, u) - 1))
                v.tensor_copy(prob_t[:, u, :, :], xr[:, u, :, D:D + 1])
                v.tensor_copy(dest_t[:, u, :, :], xr_i[:, u, :, D + 1:D + 2]).then_inc(s_taken, 1)
                v.tensor_copy(w1_t[:, u % 2, :], w1_s[:, bass.ds(e * WE, WE)]).then_inc(s_w1t, 1)

            def scale_y(s, u):
                for n in range(HALVES):
                    dve.wait_ge(s_l2, HALVES * s + n + 1)
                    if n == 0 and not (static(s) and s < 2):
                        dve.wait_ge(s_sc[(u - 2) % U], 16 * HALVES * rounds(s - 2, (u - 2) % U))
                    v.tensor_scalar(yo[:, u % 2, n, :], bank[6 + n][:, 0:D], prob_t[:, u, n, :], None,
                                    ALU.mult).then_inc(s_yo, 1)

            def expert_of(s):
                return dve.value_load(tab_e[0:1, bass.ds(s, 1)], min_val=0, max_val=NE - 1)

            def step(s, u):
                if not static(s) or s + 1 < TILES:
                    prepare(s + 1, (u + 1) % U, expert_of(s + 1))
                if not static(s) or s >= 1:
                    scale_y(s - 1, (u - 1) % U)

            dve.wait_ge(s_w1, 16 * NE)
            dve.wait_ge(s_tab, 1)
            prepare(0, 0, expert_of(0))
            expert_steps(dve, step, TILES + 1)

            for g in range(NG):
                b = g // GPB
                dve.wait_ge(s_y01[g], 16 * TOPK)
                f0 = y01[g][:, 0, :, :]
                link(v.tensor_tensor(f0, f0, y01[g][:, 1, :, :], ALU.add))
                link(v.tensor_tensor(f0, f0, gbB[:, b, :].unsqueeze(1).to_broadcast([P, GT, D]), ALU.mult))
                v.tensor_tensor(f0, f0, xs[:, tiles(g), :], ALU.add).then_inc(s_fin, 1)

        @block.tensor
        def _(pe):
            t = nc.tensor

            def transpose_group(dst, src):
                for j in range(GT):
                    ins = t.transpose(dst[:, j * P:(j + 1) * P], src(j), ident[:, :])
                return ins

            def modulation(_):
                pe.wait_ge(s_ident, 1)
                pe.wait_ge(s_small, 64)
                t.transpose(bank[7][:, 0:NSM], small[:, :], ident[0:NSM, 0:NSM]).then_inc(s_turned, 1)
                pe.wait_ge(s_cs, 1)
                pe.wait_ge(s_wmod, 16)
                for i in range(6):
                    ins = t.matmul(bank[6][:, i * B:(i + 1) * B], wmod_s[:, i * D:(i + 1) * D], csil[:, 0, :],
                                   start=True, stop=True)
                ins.then_inc(s_modc, 1)

            def modulation_rows(_):
                pe.wait_ge(s_modok, 1)
                for b in range(B):
                    ins = t.matmul(bank[6 + b][:, 0:3 * D], csil_b[:, b, :], wmod_s[:, 3 * D:6 * D],
                                   start=True, stop=True)
                pe.wait_ge(s_rw, 48)
                pe.wait_ge(s_const, 5)
                ins = t.matmul(bank[6][:, 3 * D:3 * D + NE], ones_row[:, :], rb2_row[:, :], start=True, stop=True)
                ins.then_inc(s_modb, 1)

            def xn_transpose(g):
                pe.wait_ge(s_xn, g + 1)
                wait_turn_bank(pe, "turn_x", g)
                transpose_group(turn_bank("turn_x", g), lambda j: xn[:, g % 2, j, :]).then_inc(s_xnT, 1)

            def gate_products(g):
                if g == 0:
                    pe.wait_ge(s_wbd, 1)
                pe.wait_ge(s_hT, g + 1)
                if g >= 2:
                    pe.wait_ge(s_ta, g - 1)
                z = 2 + 2 * (g % 2)
                t.matmul(bank[z][:, :], wx_bd[:, :], hT[:, cols(g)], start=True, stop=True)
                t.matmul(bank[z + 1][:, :], wa_bd[:, :], hT[:, cols(g)], start=True, stop=True).then_inc(s_z, 1)

            def y_transpose(g):
                pe.wait_ge(s_y, g + 1)
                wait_turn_bank(pe, "turn_y", g)
                transpose_group(turn_bank("turn_y", g),
                                lambda j: yv[:, g * G + j * P:g * G + (j + 1) * P]).then_inc(s_yT, 1)

            def h2_transpose(g):
                pe.wait_ge(s_h2, g + 1)
                wait_turn_bank(pe, "turn_h", g)
                transpose_group(turn_bank("turn_h", g), lambda j: rows[:, g * GT + j, 0, 0:D]).then_inc(s_h2t, 1)

            def router(g):
                if g == 0:
                    pe.wait_ge(s_rw, 48)
                    pe.wait_ge(s_ta, NG)
                pe.wait_ge(s_h2T, g + 1)
                for h in range(HC):
                    n = HC * g + h
                    if n >= HC:
                        pe.wait_ge(s_hr, n - HC + 1)
                    t.matmul(bank[2 + h][:, :], rw1_s[:, h * P:(h + 1) * P], h2T[:, g % 2, :],
                             start=True, stop=True).then_inc(s_rl1, 1)

            def logits(g):
                pe.wait_ge(s_hr, HC * (g + 1))
                if g == 0:
                    pe.wait_ge(s_modrow, 1)
                else:
                    pe.wait_ge(s_lgc, g)
                for j in range(GT):
                    for h in range(HC):
                        ins = t.matmul(bank[6][:, j * NE:(j + 1) * NE], hr[g % 2][:, h, j * P:(j + 1) * P],
                                       rw2_s[:, h, :], start=(h == 0), stop=(h == HC - 1))
                ins.then_inc(s_lg, 1)

            def ranks(g):
                pe.wait_ge(s_mask, g + 1)
                if g >= 1:
                    pe.wait_ge(s_slot, g)
                for j in range(GT):
                    o = bank[7][:, j * NE:(j + 1) * NE]
                    t.matmul(o, ones_row[:, :], ereg[:, :], start=True, stop=False)
                    for i in range(j + 1):
                        t.matmul(o, ones_bf[:, :], mboth[:, g, i, :], start=False, stop=False)
                    ins = t.matmul(o, before[:, :], mboth[:, g, j + 1, :], start=False, stop=True)
                ins.then_inc(s_pos, 1)

            run("tensor", {"setup": modulation, "modrow": modulation_rows, "turn_x": xn_transpose,
                           "gates": gate_products, "turn_y": y_transpose, "turn_h": h2_transpose,
                           "router": router, "logits": logits, "rank": ranks})
            pe.wait_ge(s_slot, NG)
            t.matmul(bank[7][:, 0:NE], ones_bf[:, :], mboth[:, NG, 0, :], start=True, stop=True).then_inc(s_cnt, 1)

            pe.wait_ge(s_w2, 16 * NE)
            pe.wait_ge(s_b2s, 16 * 3)
            pe.wait_ge(s_tab, 1)

            def turn_x(s, u):
                pe.wait_ge(s_xr[u], 16 * rounds(s, u))
                if not (static(s) and s < 2):
                    pe.wait_ge(s_xT, s - 1)
                for n in range(HALVES):
                    ins = t.transpose(bank[u % 2][:, n * P:(n + 1) * P], xr[:, u, n, 0:D], ident[:, :])
                ins.then_inc(s_txp, 1)

            def layer1(s, u):
                pe.wait_ge(s_w1t, s + 1)
                for h in range(HC):
                    if h % 2 == 0 and not (static(s) and s < 2):
                        pe.wait_ge(s_hs, 2 * (s - 2) + h // 2 + 1)
                    ins = t.matmul(bank[2 + 2 * (u % 2) + h // 2][:, (h % 2) * SL:(h % 2 + 1) * SL],
                                   w1_t[:, u % 2, h * P:(h + 1) * P], xT[:, u % 2, :], start=True, stop=True)
                    if h % 2:
                        ins.then_inc(s_l1, 1)

            def layer2(s, u, e):
                pe.wait_ge(s_hs, 2 * (s + 1))
                for n in range(HALVES):
                    if not (static(s) and s < 1):
                        pe.wait_ge(s_yo, HALVES * (s - 1) + n + 1)
                    o = bank[6 + n][:, 0:D]
                    for h in range(HC):
                        t.matmul(o, hsT[:, u % 2, h, n * P:(n + 1) * P], w2_s[:, bass.ds(e * (HC * D) + h * D, D)],
                                 start=(h == 0), stop=False)
                    t.matmul(o, ones_bf[0:3, :], b2_s[:, bass.ds(e * D, D)], start=False, stop=True).then_inc(s_l2, 1)

            def expert_of(s):
                return pe.value_load(tab_e[0:1, bass.ds(s, 1)], min_val=0, max_val=NE - 1)

            turn_x(0, 0)

            def step(s, u):
                if not static(s) or s + 1 < TILES:
                    turn_x(s + 1, (u + 1) % U)
                if not static(s) or s < TILES:
                    layer1(s, u)
                if not static(s) or s >= 1:
                    layer2(s - 1, (u - 1) % U, expert_of(s - 1))

            expert_steps(pe, step, TILES + 1)


_INS = ['L0_attn_x', 'L0_attn_a_param', 'L0_attn_w_in', 'L0_attn_w_a', 'L0_ffn_rw1', 'L0_ffn_rb1', 'L0_ffn_rw2',
        'L0_ffn_rb2', 'L0_ffn_w1', 'L0_ffn_b1', 'L0_ffn_w2', 'L0_ffn_b2', 'L0_c', 'L0_wmod']
_OUTS = [((2, 2048, 128), 'float32')]


def kernel(**inputs):
    import numpy as _np
    import concourse.bacc as _bacc
    from concourse import mybir as _mybir
    from concourse.bass_utils import run_bass_kernel_spmd as _run

    nc = _bacc.Bacc("TRN2", target_bir_lowering=False, num_devices=1)
    arrays, args = {}, []
    for name in _INS:
        a = _np.ascontiguousarray(inputs[name])
        arrays[f"in_{name}_dram"] = a
        args.append(nc.dram_tensor(f"in_{name}_dram", a.shape, _mybir.dt.from_np(a.dtype), kind="ExternalInput").ap())
    for i, (shape, dtype) in enumerate(_OUTS):
        dt = _mybir.dt.from_np(_np.dtype(dtype))
        args.append(nc.dram_tensor(f"out_{i}_dram", shape, dt, kind="ExternalOutput").ap())
    adaln_block(nc, *args)
    r = _run(nc, [arrays], core_ids=[0])
    got = tuple(r.results[0][f"out_{i}_dram"] for i in range(len(_OUTS)))
    return got[0]
```
